# Optimizing a Trainium2 kernel written in Bass

```python
import numpy as np
import jax
import jax.numpy as jnp

def _softmax(x, axis=-1):
    return jax.nn.softmax(x, axis=axis)

def _gelu(x):
    return jax.nn.gelu(x, approximate=True)

def _silu(x):
    return jax.nn.silu(x)

def _sigmoid(x):
    return jax.nn.sigmoid(x)

def _layernorm(x, axis=-1, eps=1e-05):
    m = jnp.mean(x, axis=axis, keepdims=True)
    v = jnp.var(x, axis=axis, keepdims=True)
    return (x - m) / jnp.sqrt(v + eps)

def _scatter_add(tgt, idx, src, axis=0):
    return tgt.at[idx].add(src)

def _segment_sum(src, seg, n):
    return jax.ops.segment_sum(src, seg, n)
kernel_name = 'mk_adj_preln_d2_adj_r2_a3723e'

def setup_inputs(seed: int=0):
    np.random.seed(seed)
    _w = jnp.asarray

    def _rec_inputs():
        import jax
        import jax.numpy as jnp
        _gk = jax.random.key(seed)
        x = -0.0003929 + 0.9999 * jax.random.normal(jax.random.fold_in(_gk, 1), (8, 1024, 512), jnp.float32)
        _a = jax.random.bernoulli(jax.random.fold_in(_gk, 2), 0.015625, (1024, 1024))
        _a = jnp.logical_or(_a, jnp.swapaxes(_a, -1, -2))
        _a = jnp.logical_or(_a, jnp.eye(1024, dtype=bool))
        _af = _a.astype(jnp.float32)
        _af = _af * jax.random.uniform(jax.random.fold_in(_gk, 3), (1024, 1024), jnp.float32, 0.05, 0.0220971)
        adj = _af
        return (x, adj)
    x, adj = _rec_inputs()

    def _L0_gnn_setup():
        import jax, jax.numpy as jnp
        import numpy as np
        B, T, D = (8, 1024, 512)
        key = jax.random.key(seed)
        k1, k2, k3 = jax.random.split(key, 3)
        x = jax.random.normal(k1, (B, T, D), dtype=jnp.float32)
        s1 = 1.0 / np.sqrt(2 * D)
        W1 = jax.random.uniform(k2, (2 * D, 2 * D), jnp.float32, -s1, s1)
        b1 = jnp.zeros((2 * D,), jnp.float32)
        W2 = jax.random.uniform(k3, (D, 2 * D), jnp.float32, -s1, s1)
        b2 = jnp.zeros((D,), jnp.float32)
        return {'x': x, 'W1': W1, 'b1': b1, 'W2': W2, 'b2': b2}
    _L0_gnn_all = _L0_gnn_setup()
    _L0_gnn_in = {k: v for k, v in _L0_gnn_all.items() if k in ('b1', 'W2', 'b2')}
    del _L0_gnn_all

    def _L1_gnn_setup():
        import jax, jax.numpy as jnp
        import numpy as np
        EPS = 1e-08

        def _row_stochastic_causal(A, causal_mask):
            A = A * causal_mask
            deg = jnp.maximum(A.sum(axis=-1, keepdims=True), EPS)
            return A / deg
        key = jax.random.key(seed)
        k = jax.random.split(key, 5)
        B, N, D = (4, 1024, 512)
        s = 1.0 / np.sqrt(D)
        h = jax.random.normal(k[0], (B, N, D), dtype=jnp.float32)
        W_lang = jax.random.normal(k[1], (D, D), dtype=jnp.float32) * s
        W_grav = jax.random.normal(k[2], (D, D), dtype=jnp.float32) * s
        W_V = jax.random.normal(k[3], (D, D), dtype=jnp.float32) * s
        W_O = jax.random.normal(k[4], (D, D), dtype=jnp.float32) * s
        causal_mask = jnp.tril(jnp.ones((N, N), dtype=jnp.float32))
        gate_logit = jnp.zeros((), jnp.float32)
        log_sigma = jnp.zeros((), jnp.float32)
        return {'h': h, 'causal_mask': causal_mask, 'W_lang': W_lang, 'W_grav': W_grav, 'W_V': W_V, 'W_O': W_O, 'gate_logit': gate_logit, 'log_sigma': log_sigma}
    _L1_gnn_all = _L1_gnn_setup()
    _L1_gnn_in = {k: v for k, v in _L1_gnn_all.items() if k in ('W_lang', 'W_grav', 'W_V', 'W_O', 'gate_logit', 'log_sigma')}
    del _L1_gnn_all
    return {'x': x, 'adj': adj, 'L0_gnn_b1': _L0_gnn_in['b1'], 'L0_gnn_W2': _L0_gnn_in['W2'], 'L0_gnn_b2': _L0_gnn_in['b2'], 'L1_gnn_W_lang': _L1_gnn_in['W_lang'], 'L1_gnn_W_grav': _L1_gnn_in['W_grav'], 'L1_gnn_W_V': _L1_gnn_in['W_V'], 'L1_gnn_W_O': _L1_gnn_in['W_O'], 'L1_gnn_gate_logit': _L1_gnn_in['gate_logit'], 'L1_gnn_log_sigma': _L1_gnn_in['log_sigma']}

def reference(x, adj, L0_gnn_b1, L0_gnn_W2, L0_gnn_b2, L1_gnn_W_lang, L1_gnn_W_grav, L1_gnn_W_V, L1_gnn_W_O, L1_gnn_gate_logit, L1_gnn_log_sigma):
    import jax
    import jax.numpy as jnp

    def _L0_gnn_ref(x, W1, b1, W2, b2):
        import jax, jax.numpy as jnp
        import numpy as np
        B, T, D = (8, 1024, 512)

        def step(memory, token):
            h = jnp.concatenate([token, memory], axis=-1)
            h = jax.nn.gelu(h @ W1.T + b1, approximate=False)
            proposed = h @ W2.T + b2
            g = jax.nn.sigmoid(proposed)
            memory = memory * (1.0 - g) + proposed * g
            return (memory, memory)
        x_t = jnp.swapaxes(x, 0, 1)
        init = jnp.zeros((x.shape[0], x.shape[2]), dtype=x.dtype)
        _, mems = jax.lax.scan(step, init, x_t)
        return jnp.swapaxes(mems, 0, 1)

    def _L1_gnn_ref(h, causal_mask, W_lang, W_grav, W_V, W_O, gate_logit, log_sigma):
        import jax, jax.numpy as jnp
        import numpy as np
        EPS = 1e-08

        def _row_stochastic_causal(A, causal_mask):
            A = A * causal_mask
            deg = jnp.maximum(A.sum(axis=-1, keepdims=True), EPS)
            return A / deg
        z_l = jnp.einsum('bnd,ed->bne', h, W_lang)
        z_g = jnp.einsum('bnd,ed->bne', h, W_grav)
        v = jnp.einsum('bnd,ed->bne', h, W_V)
        N = h.shape[-2]
        not_eye = 1.0 - jnp.eye(N, dtype=h.dtype)
        zn = z_l / jnp.maximum(jnp.linalg.norm(z_l, axis=-1, keepdims=True), EPS)
        A_l = jnp.maximum(jnp.einsum('bnd,bmd->bnm', zn, zn), 0.0) * not_eye
        sq = jnp.sum(z_g * z_g, axis=-1, keepdims=True)
        d2 = jnp.maximum(sq + jnp.swapaxes(sq, -1, -2) - 2.0 * jnp.einsum('bnd,bmd->bnm', z_g, z_g), 0.0)
        sigma = jnp.exp(log_sigma)
        A_g = jnp.exp(-d2 / (2.0 * sigma * sigma)) * not_eye
        K_l = _row_stochastic_causal(A_l, causal_mask)
        K_g = _row_stochastic_causal(A_g, causal_mask)
        w_l = jax.nn.sigmoid(gate_logit)
        K = w_l * K_l + (1.0 - w_l) * K_g
        out = jnp.einsum('bnm,bmd->bnd', K, v)
        return jnp.einsum('bnd,ed->bne', out, W_O)
    h = jnp.maximum(_layernorm(x, axis=-1), 0.0)
    x = x + _L0_gnn_ref(h, adj, L0_gnn_b1, L0_gnn_W2, L0_gnn_b2)
    h = jnp.maximum(_layernorm(x, axis=-1), 0.0)
    x = x + _L1_gnn_ref(h, adj, L1_gnn_W_lang, L1_gnn_W_grav, L1_gnn_W_V, L1_gnn_W_O, L1_gnn_gate_logit, L1_gnn_log_sigma)
    return x

_drawn_inputs = setup_inputs


def setup_inputs(seed=0):
    import zlib

    import numpy as np

    out = dict(_drawn_inputs(seed))
    spreads = {'L0_gnn_b1': (0.0, 0.1), 'L0_gnn_b2': (0.0, 0.1)}
    factors = {}
    for name, (base, spread) in spreads.items():
        noise = np.random.default_rng([zlib.crc32(name.encode()), seed]).standard_normal(out[name].shape)
        drawn = base * np.exp(spread * noise) if base else spread * noise
        out[name] = jnp.asarray(drawn.astype(out[name].dtype))
    for name, factor in factors.items():
        out[name] = (out[name] * factor).astype(out[name].dtype)
    return out
```

```python
from contextlib import ExitStack

import concourse.bass as bass
import concourse.mybir as mybir
from concourse.alu_op_type import AluOpType as ALU

F32 = mybir.dt.float32
F16 = mybir.dt.float16
BF16 = mybir.dt.bfloat16
I32 = mybir.dt.int32
ACT = mybir.ActivationFunctionType
AX = mybir.AxisListType

P = 128
B, T, D = 8, 1024, 512
H = 2 * D
KD, KH = D // P, H // P
CH = 64
NCH = T // CH
JT = CH * B // P
STEPS_J = P // B
NT = T // P
PARTS = 3
SLOTS = PARTS + 1
LN_EPS = 1e-5
EPS = 1e-8
EXP_MASK = 0x7F800000
RSQRT_SEED = float(0x5F3759DF)


def rsqrt(dve, link, x, y, t):
    xi, yi = x.bitcast(I32), y.bitcast(I32)
    link(dve.tensor_single_scalar(yi, xi, 1, ALU.logical_shift_right))
    link(dve.tensor_scalar(yi, yi, -1.0, RSQRT_SEED, ALU.mult, ALU.add))
    for _ in range(4):
        link(dve.scalar_tensor_tensor(t, y, -0.5, y, ALU.mult, ALU.mult))
        link(dve.tensor_tensor(t, t, x, ALU.mult))
        link(dve.scalar_tensor_tensor(y, t, 1.5, y, ALU.add, ALU.mult))


def build(nc, x, adj, b1, W2, b2, W_lang, W_grav, W_V, W_O, gate_logit, log_sigma, out):
    ctx = ExitStack()
    with ctx:
        x1 = nc.dram_tensor("x1", (B, T, D), F32, kind="Internal").ap()

        def sb(stack, name, shape, dt=F32):
            return stack.enter_context(nc.sbuf_tensor(name, shape, dt))

        def sem(name):
            return ctx.enter_context(nc.semaphore(name))

        psum = ctx.enter_context(nc.psum_tensor("psum", [P, 8, 512], F32))
        bank = [psum[:, i, :] for i in range(8)]
        ident = sb(ctx, "ident", [P, P])
        off_diag = sb(ctx, "off_diag", [P, P])
        ones = sb(ctx, "ones", [P, P])

        rec = ctx.enter_context(ExitStack())
        w1m = [sb(rec, f"w1m_{n}", [P, KD, H], F16) for n in ("hi", "lo")]
        w2t = [sb(rec, f"w2t_{n}", [P, KH, D], F16) for n in ("hi", "lo")]
        w1t = sb(rec, "w1t", [P, KD, H])
        b1c = sb(rec, "b1c", [P, KH])
        b2c = sb(rec, "b2c", [P, KD])
        scl = sb(rec, "scl", [P, 8])
        S1, S2 = scl[:, 2:3], scl[:, 3:4]
        KAPPA = scl[:, 4:5]
        SIGMA = scl[:, 5:6]
        TWO_W = scl[:, 6:8]
        mem = sb(rec, "mem", [P, KD, B, PARTS])
        MEM_AT = (2, 0, 1)
        hid = sb(rec, "hid", [P, KH, PARTS, B])
        mem_hi = mem[:, :, :, :].rearrange("p k b s -> p (k b s)").bitcast(BF16).rearrange(
            "p (k b s two) -> p k s b two", b=B, s=PARTS, two=2)[:, :, :, :, 1]
        hid_hi = hid[:, :, :, :].rearrange("p k s b -> p (k s b)").bitcast(BF16).rearrange(
            "p (k s b two) -> p k s b two", b=B, s=PARTS, two=2)[:, :, :, :, 1]
        prod = sb(rec, "prod", [P, KD, B])
        pre_sum = sb(rec, "pre_sum", [P, KH, B])
        factors = sb(rec, "factors", [P, KD, B, PARTS])
        addends = sb(rec, "addends", [P, KD, B, PARTS])

        y_bank, p_bank = bank[0:2], bank[2:4]
        y_ps = [b[:, 0:KH // 2 * SLOTS * B].rearrange("p (m s b) -> p m s b", s=SLOTS, b=B) for b in y_bank]
        p_ps = [b[:, 0:KD // 2 * SLOTS * B].rearrange("p (m s b) -> p m s b", s=SLOTS, b=B) for b in p_bank]

        adj_in, w2_in, bias_in = sem("adj_in"), sem("w2_in"), sem("bias_in")
        const_set, const_ready = sem("const_set"), sem("const_ready")
        wmax_ready, wmax_all, scales_ready = sem("wmax_ready"), sem("wmax_all"), sem("scales_ready")
        wt_ps_ready, wt_hi_done, wt_done = sem("wt_ps_ready"), sem("wt_hi_done"), sem("wt_done")
        dve_link = sem("dve_link")

        with ExitStack() as tmp:
            adj_sb = sb(tmp, "adj_sb", [P, KH, H])
            w2_sb = sb(tmp, "w2_sb", [P, KD, H])
            wmax = sb(tmp, "wmax", [P, 2])
            jobs = ([("w1t", k, m) for k in range(KD) for m in (0, 4)]
                    + [("w1m", k, m) for k in range(KD) for m in (0, 4)]
                    + [("w2", k, 0) for k in range(KH)])
            block = tmp.enter_context(nc.Block())

            @block.sync
            def _(sp):
                sp.dma_start(adj_sb[:, :, :], adj.rearrange("(m p) k -> p m k", p=P)).then_inc(adj_in, 16)
                sp.dma_start(w2_sb[:, :, :], W2.rearrange("(m p) k -> p m k", p=P)).then_inc(w2_in, 16)
                with nc.allow_non_contiguous_dma(reason="1536 words, once"):
                    sp.dma_start(b1c[:, :], b1.rearrange("(m p) -> p m", p=P)).then_inc(bias_in, 16)
                    sp.dma_start(b2c[:, :], b2.rearrange("(m p) -> p m", p=P)).then_inc(bias_in, 16)

            @block.gpsimd
            def _(pool):
                pool.memset(ident[:, :], 0.0).then_inc(const_set, 1)
                pool.memset(ones[:, :], 1.0).then_inc(const_set, 1)
                pool.wait_ge(const_set, 2)
                pool.affine_select(ident[:, :], ident[:, :], [[-1, P]], ALU.not_equal, 1.0, base=0,
                                   channel_multiplier=1).then_inc(const_ready, 1)
                pool.affine_select(off_diag[:, :], ones[:, :], [[-1, P]], ALU.not_equal, 0.0, base=0,
                                   channel_multiplier=1).then_inc(const_ready, 1)
                pool.wait_ge(wmax_ready, 2)
                pool.partition_all_reduce(TWO_W, wmax[:, :], P, bass.bass_isa.ReduceOp.absmax).then_inc(wmax_all, 1)

            @block.tensor
            def _(pe):
                pe.wait_ge(const_ready, 2)
                pe.wait_ge(adj_in, 16)
                for n, (what, k, m) in enumerate(jobs):
                    if what == "w2" and k == 0:
                        pe.wait_ge(w2_in, 16)
                    if n >= 8:
                        pe.wait_ge(wt_done, n - 7)
                    for i in range(4):
                        src = w2_sb[:, i, k * P:(k + 1) * P] if what == "w2" else \
                            adj_sb[:, m + i, (k + KD * (what == "w1m")) * P:(k + 1 + KD * (what == "w1m")) * P]
                        last = nc.tensor.transpose(bank[n % 8][:, i * P:(i + 1) * P], src, ident[:, :])
                    last.then_inc(wt_ps_ready, 1)

            @block.vector
            def _(dve):
                n_link = [0]

                def link(ins):
                    n_link[0] += 1
                    ins.then_inc(dve_link, 1)
                    dve.wait_ge(dve_link, n_link[0])

                dve.wait_ge(adj_in, 16)
                nc.vector.tensor_reduce(wmax[:, 0:1], adj_sb[:, :, :], AX.XY, ALU.max,
                                        apply_absolute_value=True).then_inc(wmax_ready, 1)
                dve.wait_ge(w2_in, 16)
                nc.vector.tensor_reduce(wmax[:, 1:2], w2_sb[:, :, :], AX.XY, ALU.max,
                                        apply_absolute_value=True).then_inc(wmax_ready, 1)
                dve.wait_ge(wmax_all, 1)
                e = TWO_W.bitcast(I32)
                s = scl[:, 2:4].bitcast(I32)
                inv = scl[:, 4:6]
                link(nc.vector.tensor_single_scalar(e, e, EXP_MASK, ALU.bitwise_and))
                link(nc.vector.tensor_scalar(e, e, float(87 << 23), None, ALU.max))
                link(nc.vector.tensor_scalar(s, e, -1.0, float(268 << 23), ALU.mult, ALU.add))
                link(nc.vector.tensor_scalar(inv.bitcast(I32), e, float(-(14 << 23)), None, ALU.add))
                link(nc.vector.tensor_tensor(KAPPA, scl[:, 4:5], scl[:, 5:6], ALU.mult))
                nc.vector.tensor_scalar(SIGMA, SIGMA, 0.5, None, ALU.mult).then_inc(scales_ready, 1)
                dve.wait_ge(scales_ready, 1)
                link(nc.vector.memset(mem[:, :, :, :], 0.0))
                link(nc.vector.memset(factors[:, :, :, :], 0.0))
                link(nc.vector.memset(factors[:, :, :, 2], 0.5))
                link(nc.vector.memset(addends[:, :, :, :], 0.0))
                for n, (what, k, m) in enumerate(jobs):
                    dve.wait_ge(wt_ps_ready, n + 1)
                    src = bank[n % 8][:, :]
                    if what == "w1t":
                        nc.vector.tensor_copy(w1t[:, k, m * P:m * P + 512], src).then_inc(wt_done, 1)
                        continue
                    parts, at, s = (w1m, m * P, S1) if what == "w1m" else (w2t, 0, S2)
                    hi, lo = (w[:, k, at:at + 512] for w in parts)
                    nc.vector.tensor_scalar(hi, src, s, None, ALU.mult).then_inc(wt_hi_done, 1)
                    dve.wait_ge(wt_hi_done, n - 7)
                    nc.vector.scalar_tensor_tensor(lo, src, s, hi, ALU.mult, ALU.subtract).then_inc(wt_done, 1)

        with ExitStack() as tmp:
            xa = sb(tmp, "xa", [P, JT, D])
            xc = sb(tmp, "xc", [P, JT, D])
            xn = sb(tmp, "xn", [P, JT, D])
            tok = sb(tmp, "tok", [P, KD, CH * B])
            pre = sb(tmp, "pre", [P, KH, (CH + 1) * B])
            hist = sb(tmp, "hist", [P, KD, CH * B])
            xo = sb(tmp, "xo", [P, JT, D])
            stats = sb(tmp, "stats", [P, JT, 6])
            mv = sb(tmp, "mv", [P, JT, 2])
            nrm = sb(tmp, "nrm", [P, 3, JT])
            table = sb(tmp, "table", [P, 1])

            x_in, xc_in, x1_out = sem("x_in"), sem("xc_in"), sem("x1_out")
            x_used, xn_ready, tok_ps_ready, tok_ready = sem("x_used"), sem("xn_ready"), sem("tok_ps_ready"), sem("tok_ready")
            pre_ps_ready, pre_ready, slot_ready = sem("pre_ps_ready"), sem("pre_ready"), sem("slot_ready")
            rows_ps_ready, xo_ready = sem("rows_ps_ready"), sem("xo_ready")
            chain = sem("chain")
            y_ready = [sem("y_ready_a"), sem("y_ready_b")]
            ysum_ready = [sem("ysum_ready_a"), sem("ysum_ready_b")]
            gelu_ready = [sem("gelu_ready_a"), sem("gelu_ready_b")]
            hid_r1 = [sem("hid_r1_a"), sem("hid_r1_b")]
            hid_ready = [sem("hid_ready_a"), sem("hid_ready_b")]
            p_ready = [sem("p_ready_a"), sem("p_ready_b")]
            psum_read = [sem("psum_read_a"), sem("psum_read_b")]
            diff_ready = [sem("diff_ready_a"), sem("diff_ready_b")]
            tanh_ready = [sem("tanh_ready_a"), sem("tanh_ready_b")]
            mem_new = [sem("mem_new_a"), sem("mem_new_b")]
            mem_r1 = [sem("mem_r1_a"), sem("mem_r1_b")]
            mem_ready = [sem("mem_ready_a"), sem("mem_ready_b")]
            slots_written = sem("slots_written")
            hist_done = sem("hist_done")
            bias_slot = sem("bias_slot")

            def rows(t, c, j):
                return t[:, bass.ds(c * CH + j * STEPS_J, STEPS_J), :].rearrange("b t d -> t b d")

            block = tmp.enter_context(nc.Block())

            @block.sync
            def _(sp):
                for j in range(JT):
                    sp.dma_start(xa[:, j, :], rows(x, 0, j)).then_inc(x_in, 16)
                with sp.Fori(0, NCH) as c:
                    sp.wait_ge(xo_ready, c * JT)
                    for j in range(JT):
                        sp.dma_start(xc[:, j, :], rows(x, c, j)).then_inc(xc_in, 16)
                    nxt = sp.snap((c + 1) % NCH)
                    sp.wait_ge(x_used, (c + 1) * JT)
                    for j in range(JT):
                        sp.dma_start(xa[:, j, :], rows(x, nxt, j)).then_inc(x_in, 16)
                    for j in range(JT):
                        sp.wait_ge(xo_ready, c * JT + j + 1)
                        sp.dma_start(rows(x1, c, j), xo[:, j, :]).then_inc(x1_out, 16)
                sp.wait_ge(x_in, 16 * JT * (NCH + 1))
                sp.wait_ge(x1_out, 16 * JT * NCH)

            @block.gpsimd
            def _(pool):
                with pool.Fori(0, NCH) as c:
                    with pool.Fori(0, CH) as t:
                        now = pool.snap(c * CH + t + 1)
                        pool.wait_ge(mem_new[0], now)
                        pool.wait_ge(mem_new[1], now)
                        pool.tensor_copy(hist[:, :, bass.ds(t * B, B)], mem[:, :, :, 2]).then_inc(hist_done, 1)

            @block.scalar
            def _(act):
                sigma = act.alloc_register("sigma")
                nc.scalar.activation(table[:, :], mem[:, 0, 0, 0:1], ACT.Gelu)
                act.reg_load(sigma, SIGMA[0:1, :].bitcast(I32))
                with act.Fori(0, NCH) as c:
                    for k in range(KD):
                        act.wait_ge(tok_ps_ready, c * KD + k + 1)
                        nc.scalar.activation(tok[:, k, :], bank[4 + k][:, :], ACT.Relu).then_inc(tok_ready, 1)
                    act.wait_ge(pre_ready, c * KH + KH)
                    for h in range(2):
                        nc.scalar.activation(y_ps[h][:, :, PARTS, :], pre[:, 4 * h:4 * h + 4, 0:B],
                                             ACT.Copy).then_inc(slots_written, 1)
                    with act.Fori(0, CH) as t:
                        now = act.snap(c * CH + t + 1)
                        for h in range(2):
                            act.wait_ge(ysum_ready[h], now)
                            nc.scalar.activation(hid[:, 4 * h:4 * h + 4, 0, :], pre_sum[:, 4 * h:4 * h + 4, :],
                                                 ACT.Gelu).then_inc(gelu_ready[h], 1)
                        for h in range(2):
                            nc.scalar.activation(y_ps[h][:, :, PARTS, :],
                                                 pre[:, 4 * h:4 * h + 4, bass.ds((t + 1) * B, B)],
                                                 ACT.Copy).then_inc(slots_written, 1)
                        for h in range(2):
                            act.wait_ge(psum_read[h], now)
                            nc.scalar.activation(factors[:, 2 * h:2 * h + 2, :, 1], prod[:, 2 * h:2 * h + 2, :],
                                                 ACT.Tanh, scale=sigma).then_inc(tanh_ready[h], 1)

            def sum_products(dve, h, now):
                dve.wait_ge(p_ready[h], now)
                nc.vector.tensor_reduce(prod[:, 2 * h:2 * h + 2, :], p_ps[h].rearrange("p m s b -> p m b s"),
                                        AX.X, ALU.add).then_inc(psum_read[h], 1)

            def update(dve, h, now):
                k = slice(2 * h, 2 * h + 2)
                value = mem[:, k, :, MEM_AT[0]]
                dve.wait_ge(psum_read[h], now)
                for at, op in enumerate((ALU.subtract, ALU.add)):
                    nc.vector.scalar_tensor_tensor(addends[:, k, :, at], prod[:, k, :], KAPPA, value,
                                                   ALU.mult, op).then_inc(diff_ready[h], 1)
                dve.wait_ge(diff_ready[h], now * 2)
                dve.wait_ge(hist_done, now - 1)
                dve.wait_ge(tanh_ready[h], now)
                nc.vector.tensor_tensor_scan(flat(mem, k), flat(factors, k), flat(addends, k), 0.0,
                                             ALU.mult, ALU.add).then_inc(mem_new[h], 1)

            def flat(t, k):
                return t[:, k, :, :].rearrange("p k b s -> p (k b s)")

            def first_rest(dve, h, now):
                k = slice(2 * h, 2 * h + 2)
                dve.wait_ge(mem_new[h], now)
                nc.vector.tensor_tensor(mem[:, k, :, MEM_AT[1]], mem[:, k, :, MEM_AT[0]],
                                        mem_hi[:, k, MEM_AT[0], :], ALU.subtract).then_inc(mem_r1[h], 1)

            def second_rest(dve, h, now):
                k = slice(2 * h, 2 * h + 2)
                dve.wait_ge(mem_r1[h], now)
                nc.vector.tensor_tensor(mem[:, k, :, MEM_AT[2]], mem[:, k, :, MEM_AT[1]],
                                        mem_hi[:, k, MEM_AT[1], :], ALU.subtract).then_inc(mem_ready[h], 1)

            @block.vector
            def _(dve):
                nlink = [0]
                at = [None]

                def link(ins):
                    nlink[0] += 1
                    ins.then_inc(chain, 1)
                    dve.wait_ge(chain, at[0] + nlink[0])

                dve.wait_ge(bias_in, 32)
                for k in range(KD):
                    nc.vector.tensor_scalar(p_ps[k // 2][:, k % 2, PARTS, :],
                                            ones[:, 0:B], b2c[:, k:k + 1], S2, ALU.mult,
                                            ALU.mult).then_inc(bias_slot, 1)
                nc.vector.memset(pre[:, :, CH * B:], 0.0).then_inc(bias_slot, 1)
                PER_CHUNK = 2 * JT + 15
                with dve.Fori(0, NCH) as c:
                    nlink[0] = 0
                    at[0] = dve.snap(c * PER_CHUNK)
                    dve.wait_ge(x_in, (c + 1) * (16 * JT))
                    for j in range(JT):
                        nc.vector.bn_stats(stats[:, j, :], xa[:, j, :]).then_inc(chain, 1)
                    nlink[0] += JT
                    dve.wait_ge(chain, at[0] + nlink[0])
                    nc.vector.memset(nrm[:, 2, :], 0.0)
                    for j in range(JT):
                        nc.vector.bn_aggr(mv[:, j, :], stats[:, j, :]).then_inc(chain, 1)
                    nlink[0] += JT
                    dve.wait_ge(chain, at[0] + nlink[0])
                    link(nc.vector.tensor_scalar(nrm[:, 0, :], mv[:, :, 1], LN_EPS, None, ALU.add))
                    rsqrt(nc.vector, link, nrm[:, 0, :], nrm[:, 1, :], nrm[:, 2, :])
                    for j in range(JT):
                        nc.vector.tensor_scalar(xn[:, j, :], xa[:, j, :], mv[:, j, 0:1], nrm[:, 1, j:j + 1],
                                                ALU.subtract, ALU.mult).then_inc(x_used, 1)
                    assert nlink[0] == PER_CHUNK
                    for m in range(KH):
                        dve.wait_ge(pre_ps_ready, c * KH + m + 1)
                        nc.vector.tensor_scalar(pre[:, m, 0:CH * B], bank[4 + m % 4][:, :], b1c[:, m:m + 1], None,
                                                ALU.add).then_inc(pre_ready, 1)
                    with dve.Fori(0, CH) as t:
                        now = dve.snap(c * CH + t + 1)
                        for h in range(2):
                            dve.wait_ge(y_ready[h], now)
                            nc.vector.tensor_reduce(pre_sum[:, 4 * h:4 * h + 4, :],
                                                    y_ps[h].rearrange("p m s b -> p m b s"),
                                                    AX.X, ALU.add).then_inc(ysum_ready[h], 1)
                        for h in range(2):
                            v = [hid[:, 4 * h:4 * h + 4, i, :] for i in range(PARTS)]
                            hi = [hid_hi[:, 4 * h:4 * h + 4, i, :] for i in range(PARTS)]
                            dve.wait_ge(gelu_ready[h], now)
                            nc.vector.tensor_tensor(v[1], v[0], hi[0], ALU.subtract).then_inc(hid_r1[h], 1)
                            dve.wait_ge(hid_r1[h], now)
                            nc.vector.tensor_tensor(v[2], v[1], hi[1], ALU.subtract).then_inc(hid_ready[h], 1)
                        sum_products(dve, 0, now)
                        update(dve, 0, now)
                        first_rest(dve, 0, now)
                        sum_products(dve, 1, now)
                        second_rest(dve, 0, now)
                        update(dve, 1, now)
                        first_rest(dve, 1, now)
                        second_rest(dve, 1, now)
                    dve.wait_ge(xc_in, (c + 1) * (16 * JT))
                    dve.wait_ge(x1_out, c * (16 * JT))
                    for j in range(JT):
                        dve.wait_ge(rows_ps_ready, c * JT + j + 1)
                        nc.vector.scalar_tensor_tensor(xo[:, j, :], bank[4 + j][:, :], S1, xc[:, j, :],
                                                       ALU.mult, ALU.add).then_inc(xo_ready, 1)

            @block.tensor
            def _(pe):
                W = PARTS * B

                def product(banks, m, per, w, parts, k, first):
                    at = (m % per) * SLOTS * B
                    for i in range(2):
                        last = nc.tensor.matmul(banks[m // per][:, at:at + W], w[i][:, k, m * P:(m + 1) * P],
                                                parts[:, k, :, :], start=first and m % per == 0 and i == 0,
                                                stop=True, skip_group_check=True)
                    return last

                pe.wait_ge(bias_slot, KD + 1)
                with pe.Fori(0, NCH) as c:
                    pe.wait_ge(x_used, (c + 1) * JT)
                    pe.wait_ge(xo_ready, c * JT)
                    for k in range(KD):
                        for j in range(JT):
                            last = nc.tensor.transpose(bank[4 + k][:, j * P:(j + 1) * P],
                                                       xn[:, j, k * P:(k + 1) * P], ident[:, :])
                        last.then_inc(tok_ps_ready, 1)
                    pe.wait_ge(tok_ready, (c + 1) * KD)
                    for m in range(KH):
                        if m >= 4:
                            pe.wait_ge(pre_ready, c * KH + m - 3)
                        for k in range(KD):
                            last = nc.tensor.matmul(bank[4 + m % 4][:, :], w1t[:, k, m * P:(m + 1) * P],
                                                    tok[:, k, :], start=k == 0, stop=k == KD - 1)
                        last.then_inc(pre_ps_ready, 1)
                    with pe.Fori(0, CH) as t:
                        g = pe.snap(c * CH + t)
                        now = pe.snap(g + 1)
                        pe.wait_ge(slots_written, (g + c) * 2 + 2)
                        pe.wait_ge(mem_ready[0], g)
                        for m in range(KH):
                            for k in (0, 1):
                                product(y_bank, m, 4, w1m, mem_hi, k, k == 0)
                        pe.wait_ge(mem_ready[1], g)
                        for h in range(2):
                            for m in range(4 * h, 4 * h + 4):
                                for k in (2, 3):
                                    last = product(y_bank, m, 4, w1m, mem_hi, k, False)
                            last.then_inc(y_ready[h], 1)
                        pe.wait_ge(hid_ready[0], now)
                        for h in range(2):
                            for m in range(2 * h, 2 * h + 2):
                                for k in range(4):
                                    product(p_bank, m, 2, w2t, hid_hi, k, k == 0)
                            if h == 0:
                                pe.wait_ge(hid_ready[1], now)
                            for m in range(2 * h, 2 * h + 2):
                                for k in range(4, 8):
                                    last = product(p_bank, m, 2, w2t, hid_hi, k, False)
                            last.then_inc(p_ready[h], 1)
                    pe.wait_ge(hist_done, (c + 1) * CH)
                    for j in range(JT):
                        for k in range(KD):
                            last = nc.tensor.transpose(bank[4 + j][:, k * P:(k + 1) * P],
                                                       hist[:, k, j * P:(j + 1) * P], ident[:, :])
                        last.then_inc(rows_ps_ready, 1)

        rec.close()
        with ExitStack() as tmp:
            xl = sb(tmp, "xl", [P, NT, D])
            rows_l = sb(tmp, "rows_l", [P, NT, D])
            rows_g = sb(tmp, "rows_g", [P, NT, D])
            hT = sb(tmp, "hT", [P, KD, T])
            zT = [sb(tmp, f"zT_{n}", [P, KD, T]) for n in "lg"]
            v = rows_l
            wT = [sb(tmp, f"wT_{n}", [P, KD, D]) for n in ("lang", "grav", "vo")]
            half_sq = sb(tmp, "half_sq", [P, T])
            A = [sb(tmp, f"A_{n}", [P, T]) for n in "lg"]
            K = sb(tmp, "K", [P, T])
            KT = sb(tmp, "KT", [P, T])
            xr = sb(tmp, "xr", [P, 2, D])
            o = sb(tmp, "o", [P, 2, D])
            stats = sb(tmp, "g_stats", [P, NT, 6])
            mv = sb(tmp, "g_mv", [P, NT, 2])
            nrm = sb(tmp, "g_nrm", [P, 3, NT])
            ss = sb(tmp, "ss", [P, 2, NT])
            adj_m = sb(tmp, "adj_m", [P, NT, T])
            coef = sb(tmp, "coef", [P, 2])
            gate = sb(tmp, "gate", [P, 8])
            WL, WG, INV_S2 = gate[:, 2:3], gate[:, 3:4], gate[:, 4:5]
            raw = [rows_l[:, 0:4, :], rows_l[:, 4:8, :], rows_g[:, 0:4, :], rows_g[:, 4:8, :]]
            woT = zT[0][:, :, 0:D]

            w_in, g_in = sem("w_in"), sem("g_in")
            gw_ps, gw_done = sem("gw_ps"), sem("gw_done")
            gexp, glink = sem("gexp"), sem("glink")
            xl_in, xr_in, o_out = sem("xl_in"), (sem("xr_in_0"), sem("xr_in_1")), (sem("o_out_0"), sem("o_out_1"))
            ln_done, hT_ps, hT_done = sem("ln_done"), sem("hT_ps"), sem("hT_done")
            z_ps = sem("z_ps")
            z_copied, z_squared = sem("z_copied"), sem("z_squared")
            zn_done, diag_done, sq_ps, sq_done = sem("zn_done"), sem("diag_done"), sem("sq_ps"), sem("sq_done")
            v_ps, v_done = sem("v_ps"), sem("v_done")
            zT_ps, zT_done = sem("zT_ps"), sem("zT_done")
            sim_l, sim_g, l_used, g_used = sem("sim_l"), sem("sim_g"), sem("l_used"), sem("g_used")
            exp_done = sem("exp_done")
            K_ready, KT_ps, KT_done = sem("K_ready"), sem("KT_ps"), sem("KT_done")
            o_ps, o_done = sem("o_ps"), sem("o_done")
            vlink, adjm_in, adjm_done = sem("vlink"), sem("adjm_in"), sem("adjm_done")
            LINKS = 47 + 5 * NT

            def out_rows(dve, b, i):
                dve.wait_ge(o_ps, b * NT + i + 1)
                dve.wait_ge(xr_in[i % 2], (b * (NT // 2) + i // 2 + 1) * 16)
                dve.wait_ge(o_out[i % 2], (b * (NT // 2) + i // 2) * 16)
                nc.vector.tensor_tensor(o[:, i % 2, :], bank[6 + i % 2][:, :], xr[:, i % 2, :], ALU.add).then_inc(o_done, 1)

            two_banks = [psum[:, 2 * z:2 * z + 2, :].rearrange("p a c -> p (a c)") for z in range(2)]

            block = tmp.enter_context(nc.Block())

            @block.sync
            def _(sp):
                for n, w in enumerate((W_lang, W_grav, W_V, W_O)):
                    sp.dma_start(raw[n], w.rearrange("(m p) k -> p m k", p=P)).then_inc(w_in, 16)
                sp.dma_start(adj_m[:, :, :], adj.rearrange("(m p) k -> p m k", p=P)).then_inc(adjm_in, 16)
                sp.dma_start(gate[:, 0:1], gate_logit.partition_broadcast(P)).then_inc(g_in, 16)
                sp.dma_start(gate[:, 1:2], log_sigma.partition_broadcast(P)).then_inc(g_in, 16)
                seq = x1.rearrange("b (n p) d -> b p n d", p=P)
                oseq = out.rearrange("b (n p) d -> b p n d", p=P)
                sp.dma_start(xl[:, :, :], seq[0]).then_inc(xl_in, 16)
                with sp.Fori(0, B) as b:
                    nxt = sp.snap((b + 1) % B)
                    sp.wait_ge(ln_done, (b + 1) * NT)
                    sp.dma_start(xl[:, :, :], seq[bass.ds(nxt, 1), :, :, :]).then_inc(xl_in, 16)
                    for i in range(NT):
                        if i >= 2:
                            sp.wait_ge(o_done, b * NT + i - 1)
                        sp.dma_start(xr[:, i % 2, :], seq[bass.ds(b, 1), :, i, :]).then_inc(xr_in[i % 2], 16)
                        if i >= 1:
                            sp.wait_ge(o_done, b * NT + i)
                            sp.dma_start(oseq[bass.ds(b, 1), :, i - 1, :], o[:, (i - 1) % 2, :]).then_inc(o_out[(i - 1) % 2], 16)
                    sp.wait_ge(o_done, b * NT + NT)
                    sp.dma_start(oseq[bass.ds(b, 1), :, NT - 1, :], o[:, (NT - 1) % 2, :]).then_inc(o_out[(NT - 1) % 2], 16)
                sp.wait_ge(xl_in, 16 * (B + 1))
                for r in range(2):
                    sp.wait_ge(o_out[r], 16 * B * NT // 2)

            @block.scalar
            def _(act):
                act.wait_ge(g_in, 32)
                nc.scalar.activation(gate[:, 2:3], gate[:, 0:1], ACT.Exp, scale=-1.0).then_inc(gexp, 1)
                nc.scalar.activation(gate[:, 4:5], gate[:, 1:2], ACT.Exp).then_inc(gexp, 1)
                with act.Fori(0, B) as b:
                    for i in range(8):
                        act.wait_ge(hT_ps, b * 8 + i + 1)
                        nc.scalar.activation(hT[:, i % 4, (i // 4) * 512:(i // 4) * 512 + 512], bank[i][:, :],
                                             ACT.Relu).then_inc(hT_done, 1)
                    for n in range(2 * NT):
                        act.wait_ge(z_ps, b * (2 * NT) + n + 1)
                        dst = (rows_l, rows_g)[n // NT][:, n % NT, :]
                        nc.scalar.activation(dst, bank[n % 8][:, :], ACT.Copy).then_inc(z_copied, 1)
                        nc.scalar.activation(bank[n % 8][:, :], bank[n % 8][:, :], ACT.Square,
                                             accum_out=ss[:, n // NT, n % NT:n % NT + 1]).then_inc(z_squared, 1)
                    for n in range(16):
                        act.wait_ge(zT_ps, b * 16 + n + 1)
                        nc.scalar.activation(zT[n // 8][:, n % 4, (n % 8 // 4) * 512:(n % 8 // 4) * 512 + 512],
                                             bank[4 + n % 4][:, :], ACT.Copy).then_inc(zT_done, 1)
                    for i in range(NT):
                        act.wait_ge(v_ps, b * NT + i + 1)
                        nc.scalar.activation(v[:, i, :], bank[i % 4][:, :], ACT.Copy).then_inc(v_done, 1)
                    for i in range(NT):
                        act.wait_ge(g_used, b * NT + i + 1)
                        nc.scalar.activation(A[1][:, :], A[1][:, :], ACT.Exp, scale=INV_S2).then_inc(exp_done, 1)
                        for q in range(2):
                            act.wait_ge(KT_ps, b * (2 * NT) + 2 * i + q + 1)
                            nc.scalar.activation(KT[:, q * 512:q * 512 + 512], bank[4 + q], ACT.Copy).then_inc(KT_done, 1)

            @block.vector
            def _(dve):
                nlink, base = [0], [0]

                def link(ins):
                    nlink[0] += 1
                    ins.then_inc(glink if base[0] is None else vlink, 1)
                    if base[0] is None:
                        dve.wait_ge(glink, nlink[0])
                    else:
                        dve.wait_ge(vlink, base[0] + nlink[0])

                base[0] = None
                dve.wait_ge(gexp, 2)
                link(nc.vector.tensor_scalar(gate[:, 2:3], gate[:, 2:3], 1.0, None, ALU.add))
                link(nc.vector.reciprocal(WL, gate[:, 2:3]))
                link(nc.vector.tensor_scalar(WG, WL, -1.0, 1.0, ALU.mult, ALU.add))
                link(nc.vector.tensor_tensor(gate[:, 4:5], gate[:, 4:5], gate[:, 4:5], ALU.mult))
                link(nc.vector.reciprocal(INV_S2, gate[:, 4:5]))
                for n in range(16):
                    dve.wait_ge(gw_ps, n + 1)
                    dst = (wT[0], wT[1], woT, wT[2])[n // 4][:, n % 4, :]
                    nc.vector.tensor_copy(dst, bank[n % 8][:, :]).then_inc(gw_done, 1)
                dve.wait_ge(adjm_in, 16)
                for i in range(NT):
                    dg = adj_m[:, i, i * P:(i + 1) * P]
                    nc.vector.tensor_tensor(dg, dg, off_diag[:, :], ALU.mult).then_inc(adjm_done, 1)
                with dve.Fori(0, B) as b:
                    nlink[0] = 0
                    base[0] = dve.snap(b * LINKS)
                    dve.wait_ge(xl_in, (b + 1) * 16)
                    for j in range(NT):
                        nc.vector.bn_stats(stats[:, j, :], xl[:, j, :]).then_inc(vlink, 1)
                    nlink[0] += NT
                    dve.wait_ge(vlink, base[0] + nlink[0])
                    nc.vector.memset(nrm[:, 2, :], 0.0)
                    for j in range(NT):
                        nc.vector.bn_aggr(mv[:, j, :], stats[:, j, :]).then_inc(vlink, 1)
                    nlink[0] += NT
                    dve.wait_ge(vlink, base[0] + nlink[0])
                    link(nc.vector.tensor_scalar(nrm[:, 0, :], mv[:, :, 1], LN_EPS, None, ALU.add))
                    rsqrt(nc.vector, link, nrm[:, 0, :], nrm[:, 1, :], nrm[:, 2, :])
                    for j in range(NT):
                        nc.vector.tensor_scalar(rows_l[:, j, :], xl[:, j, :], mv[:, j, 0:1], nrm[:, 1, j:j + 1],
                                                ALU.subtract, ALU.mult).then_inc(ln_done, 1)
                    dve.wait_ge(z_squared, b * (2 * NT) + 2 * NT)
                    link(nc.vector.tensor_scalar(nrm[:, 0, :], ss[:, 0, :], EPS * EPS, None, ALU.max))
                    rsqrt(nc.vector, link, nrm[:, 0, :], nrm[:, 1, :], nrm[:, 2, :])
                    for j in range(NT):
                        nc.vector.tensor_scalar(rows_l[:, j, :], rows_l[:, j, :], nrm[:, 1, j:j + 1], None,
                                                ALU.mult).then_inc(zn_done, 1)
                    link(nc.vector.tensor_scalar(ss[:, 1, :], ss[:, 1, :], -0.5, None, ALU.mult))
                    for j in range(NT):
                        nc.vector.tensor_scalar(K[:, j * P:(j + 1) * P], ident[:, :], ss[:, 1, j:j + 1], None,
                                                ALU.mult).then_inc(diag_done, 1)
                    for q in range(2):
                        dve.wait_ge(sq_ps, b * 2 + q + 1)
                        nc.vector.tensor_copy(half_sq[:, q * 512:q * 512 + 512], bank[4 + q][:, :]).then_inc(sq_done, 1)
                    dve.wait_ge(sq_done, b * 2 + 2)
                    dve.wait_ge(adjm_done, NT)
                    for i in range(NT):
                        dve.wait_ge(K_ready, b * NT + i)
                        dve.wait_ge(sim_l, b * NT + i + 1)
                        nc.vector.scalar_tensor_tensor(A[0][:, :], two_banks[0], 0.0, adj_m[:, i, :], ALU.max, ALU.mult,
                                                       accum_out=coef[:, 0:1]).then_inc(l_used, 1)
                        dve.wait_ge(sim_g, b * NT + i + 1)
                        nc.vector.scalar_tensor_tensor(A[1][:, :], two_banks[1], ss[:, 1, i:i + 1], half_sq[:, :],
                                                       ALU.add, ALU.add).then_inc(g_used, 1)
                        dve.wait_ge(exp_done, b * NT + i + 1)
                        dve.wait_ge(l_used, b * NT + i + 1)
                        link(nc.vector.scalar_tensor_tensor(A[1][:, :], A[1][:, :], 1.0, adj_m[:, i, :], ALU.min,
                                                            ALU.mult, accum_out=coef[:, 1:2]))
                        link(nc.vector.tensor_scalar(coef[:, :], coef[:, :], EPS, None, ALU.max))
                        link(nc.vector.reciprocal(coef[:, :], coef[:, :]))
                        link(nc.vector.tensor_tensor(coef[:, :], coef[:, :], gate[:, 2:4], ALU.mult))
                        link(nc.vector.tensor_scalar(A[0][:, :], A[0][:, :], coef[:, 0:1], None, ALU.mult))
                        dve.wait_ge(KT_done, b * (2 * NT) + 2 * i)
                        nc.vector.scalar_tensor_tensor(K[:, :], A[1][:, :], coef[:, 1:2], A[0][:, :],
                                                       ALU.mult, ALU.add).then_inc(K_ready, 1)
                        if i:
                            out_rows(dve, b, i - 1)
                    out_rows(dve, b, NT - 1)
                    assert nlink[0] == LINKS, nlink[0]

            @block.tensor
            def _(pe):
                def mm(dst, pairs):
                    for n, (l, r) in enumerate(pairs):
                        last = nc.tensor.matmul(dst, l, r, start=n == 0, stop=n == len(pairs) - 1)
                    return last

                pe.wait_ge(w_in, 64)
                for n in range(12):
                    if n >= 8:
                        pe.wait_ge(gw_done, n - 7)
                    src, k = raw[(0, 1, 3)[n // 4]], n % 4
                    for m in range(KD):
                        last = nc.tensor.transpose(bank[n % 8][:, m * P:(m + 1) * P], src[:, m, k * P:(k + 1) * P],
                                                   ident[:, :])
                    last.then_inc(gw_ps, 1)
                pe.wait_ge(gw_done, 12)
                for m in range(KD):
                    mm(bank[(12 + m) % 8][:, :], [(raw[2][:, k, m * P:(m + 1) * P], woT[:, k, :])
                                                  for k in range(KD)]).then_inc(gw_ps, 1)
                pe.wait_ge(gw_done, 16)
                with pe.Fori(0, B) as b:
                    pe.wait_ge(o_done, b * NT)
                    for i in range(8):
                        if i == 0:
                            pe.wait_ge(ln_done, b * NT + 4)
                        if i == 4:
                            pe.wait_ge(ln_done, b * NT + 8)
                        for j in range(4):
                            r = (i // 4) * 4 + j
                            last = nc.tensor.transpose(bank[i][:, j * P:(j + 1) * P],
                                                       rows_l[:, r, (i % 4) * P:(i % 4 + 1) * P], ident[:, :])
                        last.then_inc(hT_ps, 1)
                    pe.wait_ge(hT_done, b * 8 + 8)
                    for n in range(2 * NT):
                        if n >= 8:
                            pe.wait_ge(z_squared, b * (2 * NT) + n - 7)
                        mm(bank[n % 8][:, :], [(hT[:, k, (n % NT) * P:(n % NT + 1) * P], wT[n // NT][:, k, :])
                                               for k in range(KD)]).then_inc(z_ps, 1)
                    pe.wait_ge(z_squared, b * (2 * NT) + 2 * NT)
                    pe.wait_ge(diag_done, b * NT + NT)
                    for q in range(2):
                        for j in range(4):
                            last = nc.tensor.matmul(bank[4 + q][:, j * P:(j + 1) * P], ones[:, :],
                                                    K[:, (4 * q + j) * P:(4 * q + j + 1) * P],
                                                    start=j == 0, stop=True, skip_group_check=True)
                        last.then_inc(sq_ps, 1)
                    pe.wait_ge(sq_done, b * 2 + 2)
                    pe.wait_ge(zn_done, b * NT + NT)
                    for n in range(16):
                        if n >= 4:
                            pe.wait_ge(zT_done, b * 16 + n - 3)
                        for j in range(4):
                            r = (n % 8 // 4) * 4 + j
                            last = nc.tensor.transpose(bank[4 + n % 4][:, j * P:(j + 1) * P],
                                                       (rows_l, rows_g)[n // 8][:, r, (n % 4) * P:(n % 4 + 1) * P],
                                                       ident[:, :])
                        last.then_inc(zT_ps, 1)
                    pe.wait_ge(zT_done, b * 16 + 16)
                    for i in range(NT):
                        if i >= 4:
                            pe.wait_ge(v_done, b * NT + i - 3)
                        mm(bank[i % 4][:, :], [(hT[:, k, i * P:(i + 1) * P], wT[2][:, k, :])
                                               for k in range(KD)]).then_inc(v_ps, 1)
                    pe.wait_ge(v_done, b * NT + NT)

                    def sims(i):
                        for z, (ready, used) in enumerate(((sim_l, l_used), (sim_g, g_used))):
                            pe.wait_ge(used, b * NT + i)
                            for q in range(2):
                                last = mm(bank[2 * z + q], [(zT[z][:, k, i * P:(i + 1) * P],
                                                             zT[z][:, k, q * 512:q * 512 + 512]) for k in range(KD)])
                            last.then_inc(ready, 1)

                    def apply(i):
                        pe.wait_ge(K_ready, b * NT + i + 1)
                        for q in range(2):
                            for j in range(4):
                                last = nc.tensor.transpose(bank[4 + q][:, j * P:(j + 1) * P],
                                                           K[:, (4 * q + j) * P:(4 * q + j + 1) * P], ident[:, :])
                            last.then_inc(KT_ps, 1)
                        pe.wait_ge(KT_done, b * (2 * NT) + 2 * i + 2)
                        if i >= 2:
                            pe.wait_ge(o_done, b * NT + i - 1)
                        mm(bank[6 + i % 2], [(KT[:, j * P:(j + 1) * P], v[:, j, :])
                                             for j in range(NT)]).then_inc(o_ps, 1)

                    sims(0)
                    for i in range(NT):
                        if i + 1 < NT:
                            sims(i + 1)
                        apply(i)


_INS = ['x', 'adj', 'L0_gnn_b1', 'L0_gnn_W2', 'L0_gnn_b2', 'L1_gnn_W_lang', 'L1_gnn_W_grav', 'L1_gnn_W_V',
        'L1_gnn_W_O', 'L1_gnn_gate_logit', 'L1_gnn_log_sigma']


def kernel(**inputs):
    import numpy as np
    import concourse.bacc as bacc
    from concourse.bass_utils import run_bass_kernel_spmd

    nc = bacc.Bacc("TRN2", target_bir_lowering=False, num_devices=1)
    arrays, args = {}, []
    for name in _INS:
        a = np.ascontiguousarray(inputs[name])
        if a.ndim == 0:
            a = a.reshape(1)
        arrays[f"in_{name}"] = a
        args.append(nc.dram_tensor(f"in_{name}", a.shape, mybir.dt.from_np(a.dtype), kind="ExternalInput").ap())
    args.append(nc.dram_tensor("out", (B, T, D), F32, kind="ExternalOutput").ap())
    build(nc, *args)
    r = run_bass_kernel_spmd(nc, [arrays], core_ids=[0])
    return r.results[0]["out"]
```

```python
from contextlib import ExitStack

import concourse.bass as bass
import concourse.mybir as mybir
from concourse.alu_op_type import AluOpType as ALU

F32 = mybir.dt.float32
F16 = mybir.dt.float16
BF16 = mybir.dt.bfloat16
I32 = mybir.dt.int32
ACT = mybir.ActivationFunctionType
AX = mybir.AxisListType

P = 128
B, T, D = 8, 1024, 512
H = 2 * D
KD, KH = D // P, H // P
CH = 64
NCH = T // CH
JT = CH * B // P
STEPS_J = P // B
NT = T // P
PARTS = 3
SLOTS = PARTS + 1
LN_EPS = 1e-5
EPS = 1e-8
EXP_MASK = 0x7F800000
RSQRT_SEED = float(0x5F3759DF)


def rsqrt(dve, link, x, y, t):
    xi, yi = x.bitcast(I32), y.bitcast(I32)
    link(dve.tensor_single_scalar(yi, xi, 1, ALU.logical_shift_right))
    link(dve.tensor_scalar(yi, yi, -1.0, RSQRT_SEED, ALU.mult, ALU.add))
    for _ in range(4):
        link(dve.scalar_tensor_tensor(t, y, -0.5, y, ALU.mult, ALU.mult))
        link(dve.tensor_tensor(t, t, x, ALU.mult))
        link(dve.scalar_tensor_tensor(y, t, 1.5, y, ALU.add, ALU.mult))


def build(nc, x, adj, b1, W2, b2, W_lang, W_grav, W_V, W_O, gate_logit, log_sigma, out):
    ctx = ExitStack()
    with ctx:
        x1 = nc.dram_tensor("x1", (B, T, D), F32, kind="Internal").ap()

        def sb(stack, name, shape, dt=F32):
            return stack.enter_context(nc.sbuf_tensor(name, shape, dt))

        def sem(name):
            return ctx.enter_context(nc.semaphore(name))

        psum = ctx.enter_context(nc.psum_tensor("psum", [P, 8, 512], F32))
        bank = [psum[:, i, :] for i in range(8)]
        ident = sb(ctx, "ident", [P, P])
        off_diag = sb(ctx, "off_diag", [P, P])
        ones = sb(ctx, "ones", [P, P])

        rec = ctx.enter_context(ExitStack())
        w1m = [sb(rec, f"w1m_{n}", [P, KD, H], F16) for n in ("hi", "lo")]
        w2t = [sb(rec, f"w2t_{n}", [P, KH, D], F16) for n in ("hi", "lo")]
        w1t = sb(rec, "w1t", [P, KD, H])
        b1c = sb(rec, "b1c", [P, KH])
        b2c = sb(rec, "b2c", [P, KD])
        scl = sb(rec, "scl", [P, 8])
        TWO_W = scl[:, 0:2]
        S1, S2 = scl[:, 2:3], scl[:, 3:4]
        INV_S12 = scl[:, 4:5]
        INV_S2 = scl[:, 5:6]
        HALF_INV_S2 = scl[:, 6:7]
        S12 = scl[:, 7:8]
        mem = sb(rec, "mem", [P, KD, B, PARTS])
        MEM_AT = (2, 0, 1)
        hid = sb(rec, "hid", [P, KH, PARTS, B])
        mem_hi = mem[:, :, :, :].rearrange("p k b s -> p (k b s)").bitcast(BF16).rearrange(
            "p (k b s two) -> p k s b two", b=B, s=PARTS, two=2)[:, :, :, :, 1]
        hid_hi = hid[:, :, :, :].rearrange("p k s b -> p (k s b)").bitcast(BF16).rearrange(
            "p (k s b two) -> p k s b two", b=B, s=PARTS, two=2)[:, :, :, :, 1]
        prod = sb(rec, "prod", [P, KD, B])
        pre_sum = sb(rec, "pre_sum", [P, KH, B])
        factors = sb(rec, "factors", [P, KD, B, PARTS])
        addends = sb(rec, "addends", [P, KD, B, PARTS])

        p_bank, y_bank = bank[0:2], bank[2:6]
        NG = 4
        GT = KH // NG
        y_ps = [b[:, 0:GT * SLOTS * B].rearrange("p (m s b) -> p m s b", s=SLOTS, b=B) for b in y_bank]
        y_slots = psum[:, 2:6, 0:GT * SLOTS * B].rearrange("p g (m s b) -> p g m s b", s=SLOTS, b=B)[:, :, :, PARTS, :]
        p_ps = [b[:, 0:KD // 2 * SLOTS * B].rearrange("p (m s b) -> p m s b", s=SLOTS, b=B) for b in p_bank]

        adj_in, w2_in, bias_in = sem("adj_in"), sem("w2_in"), sem("bias_in")
        const_set, const_ready = sem("const_set"), sem("const_ready")
        wmax_ready, wmax_all = sem("wmax_ready"), sem("wmax_all")
        wt_ps_ready, wt_hi_done, wt_done = sem("wt_ps_ready"), sem("wt_hi_done"), sem("wt_done")
        dve_link = sem("dve_link")

        with ExitStack() as tmp:
            adj_sb = sb(tmp, "adj_sb", [P, KH, H])
            w2_sb = sb(tmp, "w2_sb", [P, KD, H])
            wmax = sb(tmp, "wmax", [P, 2])
            jobs = ([("w1t", k, m) for k in range(KD) for m in (0, 4)]
                    + [("w1m", k, m) for k in range(KD) for m in (0, 4)]
                    + [("w2", k, 0) for k in range(KH)])
            block = tmp.enter_context(nc.Block())

            @block.sync
            def _(sp):
                sp.dma_start(adj_sb[:, :, :], adj.rearrange("(m p) k -> p m k", p=P)).then_inc(adj_in, 16)
                sp.dma_start(w2_sb[:, :, :], W2.rearrange("(m p) k -> p m k", p=P)).then_inc(w2_in, 16)
                with nc.allow_non_contiguous_dma(reason="1536 words, once"):
                    sp.dma_start(b1c[:, :], b1.rearrange("(m p) -> p m", p=P)).then_inc(bias_in, 16)
                    sp.dma_start(b2c[:, :], b2.rearrange("(m p) -> p m", p=P)).then_inc(bias_in, 16)

            @block.gpsimd
            def _(pool):
                pool.memset(ident[:, :], 0.0).then_inc(const_set, 1)
                pool.memset(ones[:, :], 1.0).then_inc(const_set, 1)
                pool.wait_ge(const_set, 2)
                pool.affine_select(ident[:, :], ident[:, :], [[-1, P]], ALU.not_equal, 1.0, base=0,
                                   channel_multiplier=1).then_inc(const_ready, 1)
                pool.affine_select(off_diag[:, :], ones[:, :], [[-1, P]], ALU.not_equal, 0.0, base=0,
                                   channel_multiplier=1).then_inc(const_ready, 1)
                pool.wait_ge(wmax_ready, 2)
                pool.partition_all_reduce(TWO_W, wmax[:, :], P, bass.bass_isa.ReduceOp.absmax).then_inc(wmax_all, 1)

            @block.tensor
            def _(pe):
                pe.wait_ge(const_ready, 2)
                pe.wait_ge(adj_in, 16)
                for n, (what, k, m) in enumerate(jobs):
                    if what == "w2" and k == 0:
                        pe.wait_ge(w2_in, 16)
                    if n >= 8:
                        pe.wait_ge(wt_done, n - 7)
                    for i in range(4):
                        src = w2_sb[:, i, k * P:(k + 1) * P] if what == "w2" else \
                            adj_sb[:, m + i, (k + KD * (what == "w1m")) * P:(k + 1 + KD * (what == "w1m")) * P]
                        last = nc.tensor.transpose(bank[n % 8][:, i * P:(i + 1) * P], src, ident[:, :])
                    last.then_inc(wt_ps_ready, 1)

            @block.vector
            def _(dve):
                n_link = [0]

                def link(ins):
                    n_link[0] += 1
                    ins.then_inc(dve_link, 1)
                    dve.wait_ge(dve_link, n_link[0])

                dve.wait_ge(adj_in, 16)
                nc.vector.tensor_reduce(wmax[:, 0:1], adj_sb[:, :, :], AX.XY, ALU.max,
                                        apply_absolute_value=True).then_inc(wmax_ready, 1)
                dve.wait_ge(w2_in, 16)
                nc.vector.tensor_reduce(wmax[:, 1:2], w2_sb[:, :, :], AX.XY, ALU.max,
                                        apply_absolute_value=True).then_inc(wmax_ready, 1)
                dve.wait_ge(wmax_all, 1)
                e = TWO_W.bitcast(I32)
                s = scl[:, 2:4].bitcast(I32)
                inv = scl[:, 4:6]
                link(nc.vector.tensor_single_scalar(e, e, EXP_MASK, ALU.bitwise_and))
                link(nc.vector.tensor_scalar(e, e, float(87 << 23), None, ALU.max))
                link(nc.vector.tensor_scalar(s, e, -1.0, float(268 << 23), ALU.mult, ALU.add))
                link(nc.vector.tensor_scalar(inv.bitcast(I32), e, float(-(14 << 23)), None, ALU.add))
                link(nc.vector.tensor_tensor(INV_S12, INV_S12, INV_S2, ALU.mult))
                link(nc.vector.tensor_scalar(HALF_INV_S2, INV_S2, 0.5, None, ALU.mult))
                link(nc.vector.tensor_tensor(S12, S1, S2, ALU.mult))
                dve.wait_ge(bias_in, 32)
                link(nc.vector.tensor_scalar(b1c[:, :], b1c[:, :], S12, None, ALU.mult))
                link(nc.vector.memset(mem[:, :, :, :], 0.0))
                link(nc.vector.memset(factors[:, :, :, :], 0.0))
                link(nc.vector.memset(factors[:, :, :, 2], 0.5))
                link(nc.vector.memset(addends[:, :, :, :], 0.0))
                for n, (what, k, m) in enumerate(jobs):
                    dve.wait_ge(wt_ps_ready, n + 1)
                    src = bank[n % 8][:, :]
                    if what == "w1t":
                        nc.vector.tensor_copy(w1t[:, k, m * P:m * P + 512], src).then_inc(wt_done, 1)
                        continue
                    parts, at, s = (w1m, m * P, S1) if what == "w1m" else (w2t, 0, S2)
                    hi, lo = (w[:, k, at:at + 512] for w in parts)
                    nc.vector.tensor_scalar(hi, src, s, None, ALU.mult).then_inc(wt_hi_done, 1)
                    dve.wait_ge(wt_hi_done, n - 7)
                    nc.vector.scalar_tensor_tensor(lo, src, s, hi, ALU.mult, ALU.subtract).then_inc(wt_done, 1)

        with ExitStack() as tmp:
            xa = sb(tmp, "xa", [P, JT, D])
            xc = sb(tmp, "xc", [P, JT, D])
            xn = sb(tmp, "xn", [P, JT, D])
            tok = sb(tmp, "tok", [P, KD, CH * B])
            pre = sb(tmp, "pre", [P, 2, KH, (CH + 1) * B])
            hist = sb(tmp, "hist", [P, KD, CH * B])
            xo = sb(tmp, "xo", [P, JT, D])
            stats = sb(tmp, "stats", [P, JT, 6])
            mv = sb(tmp, "mv", [P, JT, 2])
            nrm = sb(tmp, "nrm", [P, 3, JT])
            table = sb(tmp, "table", [P, 1])

            x_in, xc_in, x1_out = sem("x_in"), sem("xc_in"), sem("x1_out")
            x_used, xn_ready, tok_ps_ready, tok_ready = sem("x_used"), sem("xn_ready"), sem("tok_ps_ready"), sem("tok_ready")
            pre_ps_ready, pre_ready, slot_ready = sem("pre_ps_ready"), sem("pre_ready"), sem("slot_ready")
            rows_ps_ready, xo_ready = sem("rows_ps_ready"), sem("xo_ready")
            chain = sem("chain")
            y_ready = [sem(f"y_ready_{g}") for g in range(NG)]
            ysum_ready = [sem(f"ysum_ready_{g}") for g in range(NG)]
            gelu_ready = [sem(f"gelu_ready_{g}") for g in range(NG)]
            hid_r1 = [sem(f"hid_r1_{g}") for g in range(NG)]
            hid_ready = [sem(f"hid_ready_{g}") for g in range(NG)]
            fill_ready, fill_done = sem("fill_ready"), sem("fill_done")
            p_ready = [sem("p_ready_a"), sem("p_ready_b")]
            psum_read = [sem("psum_read_a"), sem("psum_read_b")]
            diff_ready = [sem("diff_ready_a"), sem("diff_ready_b")]
            tanh_ready = [sem("tanh_ready_a"), sem("tanh_ready_b")]
            mem_new = [sem("mem_new_a"), sem("mem_new_b")]
            mem_r1 = [sem("mem_r1_a"), sem("mem_r1_b")]
            mem_ready = [sem("mem_ready_a"), sem("mem_ready_b")]
            slots_written = sem("slots_written")
            hist_done = sem("hist_done")
            bias_slot = sem("bias_slot")

            FK = KD
            FW = CH * B // 2
            FPIECE = FW // FK
            FILLS = 2 * KH
            PRE_T = (CH + 1) * B
            pre_pieces = pre[:, :, :, :].rearrange("p a m t -> p (a m t)")
            psum_flat = psum[:, :, :].rearrange("p a c -> p (a c)")

            def rows(t, c, j):
                return t[:, bass.ds(c * CH + j * STEPS_J, STEPS_J), :].rearrange("b t d -> t b d")

            block = tmp.enter_context(nc.Block())

            @block.sync
            def _(sp):
                for first in range(2):
                    sp.wait_ge(x_used, first * JT)
                    for j in range(JT):
                        sp.dma_start(xa[:, j, :], rows(x, first, j)).then_inc(x_in, 16)
                with sp.Fori(0, NCH) as c:
                    sp.wait_ge(xo_ready, c * JT)
                    for j in range(JT):
                        sp.dma_start(xc[:, j, :], rows(x, c, j)).then_inc(xc_in, 16)
                    nxt = sp.snap((c + 2) % NCH)
                    sp.wait_ge(x_used, (c + 2) * JT)
                    for j in range(JT):
                        sp.dma_start(xa[:, j, :], rows(x, nxt, j)).then_inc(x_in, 16)
                    for j in range(JT):
                        sp.wait_ge(xo_ready, c * JT + j + 1)
                        sp.dma_start(rows(x1, c, j), xo[:, j, :]).then_inc(x1_out, 16)
                sp.wait_ge(x_in, 16 * JT * (NCH + 2))
                sp.wait_ge(x1_out, 16 * JT * NCH)

            @block.gpsimd
            def _(pool):
                with pool.Fori(0, NCH) as c:
                    with pool.Fori(0, CH) as t:
                        now = pool.snap(c * CH + t + 1)
                        pool.wait_ge(mem_new[0], now)
                        pool.wait_ge(mem_new[1], now)
                        pool.tensor_copy(hist[:, :, bass.ds(t * B, B)], mem[:, :, :, 2]).then_inc(hist_done, 1)

            @block.scalar
            def _(act):
                half_inv_s2, inv_s12, s12 = (act.alloc_register(n) for n in ("half_inv_s2", "inv_s12", "s12"))
                nc.scalar.activation(table[:, :], mem[:, 0, 0, 0:1], ACT.Gelu)
                act.reg_load(half_inv_s2, HALF_INV_S2[0:1, :].bitcast(I32))
                act.reg_load(inv_s12, INV_S12[0:1, :].bitcast(I32))
                act.reg_load(s12, S12[0:1, :].bitcast(I32))

                def take_tokens(n):
                    for k in range(KD):
                        act.wait_ge(tok_ps_ready, n * KD + k + 1)
                        nc.scalar.activation(tok[:, k, :], bank[2 + k][:, :], ACT.Relu).then_inc(tok_ready, 1)

                take_tokens(0)
                with act.Fori(0, NCH) as c:
                    now_pre = pre[:, bass.ds(c % 2, 1), :, :].rearrange("p a (g m) t -> p (a g) m t", g=NG)
                    act.wait_ge(fill_ready, c * FILLS + 1)
                    take_tokens(c + 1)
                    act.wait_ge(pre_ready, KH)
                    act.wait_ge(tok_ready, (c + 2) * KD)
                    act.wait_ge(fill_done, c * CH)
                    nc.scalar.activation(y_slots, now_pre[:, :, :, 0:B], ACT.Copy).then_inc(slots_written, 1)
                    with act.Fori(0, CH) as t:
                        now = act.snap(c * CH + t + 1)
                        for g in range(NG):
                            act.wait_ge(ysum_ready[g], now)
                            nc.scalar.activation(hid[:, GT * g:GT * g + GT, 0, :], pre_sum[:, GT * g:GT * g + GT, :],
                                                 ACT.Gelu, scale=inv_s12).then_inc(gelu_ready[g], 1)
                        act.wait_ge(fill_done, c * CH + t)
                        nc.scalar.activation(y_slots, now_pre[:, :, :, bass.ds((t + 1) * B, B)],
                                             ACT.Copy).then_inc(slots_written, 1)
                        g = act.snap(c * CH + t + CH - FK)
                        q = act.snap(g % CH)
                        act.wait_ge(fill_ready, (c * CH + t) // FK + 1)
                        nc.scalar.activation(
                            pre_pieces[:, bass.ds((g // CH) % 2 * (KH * PRE_T) + q // (CH // KH) * PRE_T
                                                  + q % (CH // KH) * FPIECE, FPIECE)],
                            psum_flat[:, bass.ds(6 * 512 + q // FK % 2 * 512 + q % FK * FPIECE, FPIECE)],
                            ACT.Identity, bias=b1c[:, bass.ds(q // (CH // KH), 1)], scale=s12).then_inc(fill_done, 1)
                        for h in range(2):
                            act.wait_ge(psum_read[h], now)
                            nc.scalar.activation(factors[:, 2 * h:2 * h + 2, :, 1], prod[:, 2 * h:2 * h + 2, :],
                                                 ACT.Tanh, scale=half_inv_s2).then_inc(tanh_ready[h], 1)

            def sum_products(dve, h, now):
                dve.wait_ge(p_ready[h], now)
                nc.vector.tensor_reduce(prod[:, 2 * h:2 * h + 2, :], p_ps[h].rearrange("p m s b -> p m b s"),
                                        AX.X, ALU.add).then_inc(psum_read[h], 1)

            def update(dve, h, now):
                k = slice(2 * h, 2 * h + 2)
                value = mem[:, k, :, MEM_AT[0]]
                dve.wait_ge(psum_read[h], now)
                for at, op in enumerate((ALU.subtract, ALU.add)):
                    nc.vector.tensor_tensor(addends[:, k, :, at], prod[:, k, :], value, op).then_inc(diff_ready[h], 1)
                dve.wait_ge(diff_ready[h], now * 2)
                dve.wait_ge(hist_done, now - 1)
                dve.wait_ge(tanh_ready[h], now)
                nc.vector.tensor_tensor_scan(flat(mem, k), flat(factors, k), flat(addends, k), 0.0,
                                             ALU.mult, ALU.add).then_inc(mem_new[h], 1)

            def flat(t, k):
                return t[:, k, :, :].rearrange("p k b s -> p (k b s)")

            def first_rest(dve, h, now):
                k = slice(2 * h, 2 * h + 2)
                dve.wait_ge(mem_new[h], now)
                nc.vector.tensor_tensor(mem[:, k, :, MEM_AT[1]], mem[:, k, :, MEM_AT[0]],
                                        mem_hi[:, k, MEM_AT[0], :], ALU.subtract).then_inc(mem_r1[h], 1)

            def second_rest(dve, h, now):
                k = slice(2 * h, 2 * h + 2)
                dve.wait_ge(mem_r1[h], now)
                nc.vector.tensor_tensor(mem[:, k, :, MEM_AT[2]], mem[:, k, :, MEM_AT[1]],
                                        mem_hi[:, k, MEM_AT[1], :], ALU.subtract).then_inc(mem_ready[h], 1)

            @block.vector
            def _(dve):
                nlink = [0]
                at = [None]

                def link(ins):
                    nlink[0] += 1
                    ins.then_inc(chain, 1)
                    dve.wait_ge(chain, at[0] + nlink[0])

                dve.wait_ge(bias_in, 32)
                for k in range(KD):
                    nc.vector.tensor_scalar(p_ps[k // 2][:, k % 2, PARTS, :],
                                            ones[:, 0:B], b2c[:, k:k + 1], S2, ALU.mult,
                                            ALU.mult).then_inc(bias_slot, 1)
                nc.vector.memset(pre[:, :, :, CH * B:], 0.0).then_inc(bias_slot, 1)
                PER_CHUNK = 2 * JT + 15

                def layer_norm(n):
                    nlink[0] = 0
                    at[0] = n * PER_CHUNK if isinstance(n, int) else dve.snap(n * PER_CHUNK)
                    dve.wait_ge(x_in, (n + 1) * (16 * JT))
                    for j in range(JT):
                        nc.vector.bn_stats(stats[:, j, :], xa[:, j, :]).then_inc(chain, 1)
                    nlink[0] += JT
                    dve.wait_ge(chain, at[0] + nlink[0])
                    nc.vector.memset(nrm[:, 2, :], 0.0)
                    for j in range(JT):
                        nc.vector.bn_aggr(mv[:, j, :], stats[:, j, :]).then_inc(chain, 1)
                    nlink[0] += JT
                    dve.wait_ge(chain, at[0] + nlink[0])
                    link(nc.vector.tensor_scalar(nrm[:, 0, :], mv[:, :, 1], LN_EPS, None, ALU.add))
                    rsqrt(nc.vector, link, nrm[:, 0, :], nrm[:, 1, :], nrm[:, 2, :])
                    assert nlink[0] == PER_CHUNK
                    dve.wait_ge(tok_ps_ready, n * KD)
                    for j in range(JT):
                        nc.vector.tensor_scalar(xn[:, j, :], xa[:, j, :], mv[:, j, 0:1], nrm[:, 1, j:j + 1],
                                                ALU.subtract, ALU.mult).then_inc(x_used, 1)

                layer_norm(0)
                for m in range(KH):
                    dve.wait_ge(pre_ps_ready, m + 1)
                    nc.vector.tensor_scalar(pre[:, 0, m, 0:CH * B], bank[2 + m % 4], S12, b1c[:, m:m + 1],
                                            ALU.mult, ALU.add).then_inc(pre_ready, 1)
                layer_norm(1)
                with dve.Fori(0, NCH) as c:
                    with dve.Fori(0, CH) as t:
                        now = dve.snap(c * CH + t + 1)

                        def take_sum(g):
                            dve.wait_ge(y_ready[g], now)
                            nc.vector.tensor_reduce(pre_sum[:, GT * g:GT * g + GT, :],
                                                    y_ps[g].rearrange("p m s b -> p m b s"),
                                                    AX.X, ALU.add).then_inc(ysum_ready[g], 1)

                        def hid_rest(g, i):
                            dve.wait_ge((gelu_ready, hid_r1)[i][g], now)
                            k = slice(GT * g, GT * g + GT)
                            nc.vector.tensor_tensor(hid[:, k, i + 1, :], hid[:, k, i, :], hid_hi[:, k, i, :],
                                                    ALU.subtract).then_inc((hid_r1, hid_ready)[i][g], 1)

                        take_sum(0)
                        take_sum(1)
                        hid_rest(0, 0)
                        take_sum(2)
                        hid_rest(0, 1)
                        hid_rest(1, 0)
                        take_sum(3)
                        hid_rest(1, 1)
                        hid_rest(2, 0)
                        hid_rest(2, 1)
                        hid_rest(3, 0)
                        hid_rest(3, 1)
                        sum_products(dve, 0, now)
                        update(dve, 0, now)
                        first_rest(dve, 0, now)
                        sum_products(dve, 1, now)
                        second_rest(dve, 0, now)
                        update(dve, 1, now)
                        first_rest(dve, 1, now)
                        second_rest(dve, 1, now)
                    dve.wait_ge(xc_in, (c + 1) * (16 * JT))
                    dve.wait_ge(x1_out, c * (16 * JT))
                    for j in range(JT):
                        dve.wait_ge(rows_ps_ready, c * JT + j + 1)
                        nc.vector.scalar_tensor_tensor(xo[:, j, :], bank[2 + j][:, :], INV_S2, xc[:, j, :],
                                                       ALU.mult, ALU.add).then_inc(xo_ready, 1)
                    layer_norm(c + 2)

            @block.tensor
            def _(pe):
                W = PARTS * B

                def product(banks, m, per, w, parts, k, first):
                    at = (m % per) * SLOTS * B
                    for i in range(2):
                        last = nc.tensor.matmul(banks[m // per][:, at:at + W], w[i][:, k, m * P:(m + 1) * P],
                                                parts[:, k, :, :], start=first and m % per == 0 and i == 0,
                                                stop=True, skip_group_check=True)
                    return last

                def give_tokens(n):
                    pe.wait_ge(x_used, (n + 1) * JT)
                    for k in range(KD):
                        for j in range(JT):
                            last = nc.tensor.transpose(bank[2 + k][:, j * P:(j + 1) * P],
                                                       xn[:, j, k * P:(k + 1) * P], ident[:, :])
                        last.then_inc(tok_ps_ready, 1)

                def fill(m, half, k):
                    at = (6 + half) * 512
                    cols = slice(at, at + FW) if isinstance(half, int) else bass.ds(at, FW)
                    src = slice(half * FW, half * FW + FW) if isinstance(half, int) else bass.ds(half * FW, FW)
                    last = nc.tensor.matmul(psum_flat[:, cols], w1t[:, k, m * P:(m + 1) * P], tok[:, k, src],
                                            start=k == 0, stop=k == KD - 1)
                    if k == KD - 1:
                        last.then_inc(fill_ready, 1)

                def step(c, mf, half, kf):
                    g = pe.snap(c * CH + half * FK + (mf * (CH // KH) + kf))
                    now = pe.snap(g + 1)
                    pe.wait_ge(slots_written, g + c + 1)
                    pe.wait_ge(mem_ready[0], g)
                    for m in range(KH):
                        for k in (0, 1):
                            product(y_bank, m, GT, w1m, mem_hi, k, k == 0)
                    pe.wait_ge(mem_ready[1], g)
                    for m in range(KH):
                        for k in (2, 3):
                            last = product(y_bank, m, GT, w1m, mem_hi, k, False)
                        if m % GT == GT - 1:
                            last.then_inc(y_ready[m // GT], 1)
                    fill(mf, half, kf)
                    for h in range(2):
                        for q in range(NG):
                            if h == 0:
                                pe.wait_ge(hid_ready[q], now)
                            for m in range(2 * h, 2 * h + 2):
                                for k in range(GT * q, GT * q + GT):
                                    last = product(p_bank, m, 2, w2t, hid_hi, k, k == 0)
                        last.then_inc(p_ready[h], 1)

                give_tokens(0)
                pe.wait_ge(tok_ready, KD)
                for m in range(KH):
                    if m >= 4:
                        pe.wait_ge(pre_ready, m - 3)
                    for k in range(KD):
                        last = nc.tensor.matmul(bank[2 + m % 4][:, :], w1t[:, k, m * P:(m + 1) * P],
                                                tok[:, k, :], start=k == 0, stop=k == KD - 1)
                    last.then_inc(pre_ps_ready, 1)
                pe.wait_ge(bias_slot, KD + 1)
                pe.wait_ge(pre_ready, KH)
                for k in range(KD):
                    fill(KH - 1, 1, k)
                with pe.Fori(0, NCH) as c:
                    pe.wait_ge(xo_ready, c * JT)
                    give_tokens(c + 1)
                    for mf in range(KH):
                        with pe.Fori(0, 2) as half:
                            for kf in range(FK):
                                step(c, mf, half, kf)
                    pe.wait_ge(hist_done, (c + 1) * CH)
                    for j in range(JT):
                        for k in range(KD):
                            last = nc.tensor.transpose(bank[2 + j][:, k * P:(k + 1) * P],
                                                       hist[:, k, j * P:(j + 1) * P], ident[:, :])
                        last.then_inc(rows_ps_ready, 1)

        rec.close()
        with ExitStack() as tmp:
            xl = sb(tmp, "xl", [P, NT, D])
            rows_l = sb(tmp, "rows_l", [P, NT, D])
            rows_g = sb(tmp, "rows_g", [P, NT, D])
            hT = sb(tmp, "hT", [P, KD, T])
            zT = [sb(tmp, f"zT_{n}", [P, KD, T]) for n in "lg"]
            v = rows_l
            wT = [sb(tmp, f"wT_{n}", [P, KD, D]) for n in ("lang", "grav", "vo")]
            half_sq = sb(tmp, "half_sq", [P, T])
            A = [sb(tmp, f"A_{n}", [P, T]) for n in "lg"]
            K = sb(tmp, "K", [P, T])
            KT = sb(tmp, "KT", [P, T])
            xr = sb(tmp, "xr", [P, 2, D])
            o = sb(tmp, "o", [P, 2, D])
            stats = sb(tmp, "g_stats", [P, NT, 6])
            mv = sb(tmp, "g_mv", [P, NT, 2])
            nrm = sb(tmp, "g_nrm", [P, 3, NT])
            ss = sb(tmp, "ss", [P, 2, NT])
            adj_m = sb(tmp, "adj_m", [P, NT, T])
            coef = sb(tmp, "coef", [P, 2])
            gate = sb(tmp, "gate", [P, 8])
            WL, WG, INV_S2 = gate[:, 2:3], gate[:, 3:4], gate[:, 4:5]
            raw = [rows_l[:, 0:4, :], rows_l[:, 4:8, :], rows_g[:, 0:4, :], rows_g[:, 4:8, :]]
            woT = zT[0][:, :, 0:D]

            w_in, g_in = sem("w_in"), sem("g_in")
            gw_ps, gw_done = sem("gw_ps"), sem("gw_done")
            gexp, glink = sem("gexp"), sem("glink")
            xl_in, xr_in, o_out = sem("xl_in"), (sem("xr_in_0"), sem("xr_in_1")), (sem("o_out_0"), sem("o_out_1"))
            ln_done, hT_ps, hT_done = sem("ln_done"), sem("hT_ps"), sem("hT_done")
            z_ps = sem("z_ps")
            z_copied, z_squared = sem("z_copied"), sem("z_squared")
            zn_done, diag_done, sq_ps, sq_done = sem("zn_done"), sem("diag_done"), sem("sq_ps"), sem("sq_done")
            v_ps, v_done = sem("v_ps"), sem("v_done")
            zT_ps, zT_done = sem("zT_ps"), sem("zT_done")
            sim_l, sim_g, l_used, g_used = sem("sim_l"), sem("sim_g"), sem("l_used"), sem("g_used")
            exp_done = sem("exp_done")
            K_ready, KT_ps, KT_done = sem("K_ready"), sem("KT_ps"), sem("KT_done")
            o_ps, o_done = sem("o_ps"), sem("o_done")
            vlink, adjm_in, adjm_done = sem("vlink"), sem("adjm_in"), sem("adjm_done")
            LINKS = 47 + 5 * NT

            def out_rows(dve, b, i):
                dve.wait_ge(o_ps, b * NT + i + 1)
                dve.wait_ge(xr_in[i % 2], (b * (NT // 2) + i // 2 + 1) * 16)
                dve.wait_ge(o_out[i % 2], (b * (NT // 2) + i // 2) * 16)
                nc.vector.tensor_tensor(o[:, i % 2, :], bank[6 + i % 2][:, :], xr[:, i % 2, :], ALU.add).then_inc(o_done, 1)

            two_banks = [psum[:, 2 * z:2 * z + 2, :].rearrange("p a c -> p (a c)") for z in range(2)]

            block = tmp.enter_context(nc.Block())

            @block.sync
            def _(sp):
                for n, w in enumerate((W_lang, W_grav, W_V, W_O)):
                    sp.dma_start(raw[n], w.rearrange("(m p) k -> p m k", p=P)).then_inc(w_in, 16)
                sp.dma_start(adj_m[:, :, :], adj.rearrange("(m p) k -> p m k", p=P)).then_inc(adjm_in, 16)
                sp.dma_start(gate[:, 0:1], gate_logit.partition_broadcast(P)).then_inc(g_in, 16)
                sp.dma_start(gate[:, 1:2], log_sigma.partition_broadcast(P)).then_inc(g_in, 16)
                seq = x1.rearrange("b (n p) d -> b p n d", p=P)
                oseq = out.rearrange("b (n p) d -> b p n d", p=P)
                sp.dma_start(xl[:, :, :], seq[0]).then_inc(xl_in, 16)
                with sp.Fori(0, B) as b:
                    nxt = sp.snap((b + 1) % B)
                    sp.wait_ge(ln_done, (b + 1) * NT)
                    sp.dma_start(xl[:, :, :], seq[bass.ds(nxt, 1), :, :, :]).then_inc(xl_in, 16)
                    for i in range(NT):
                        if i >= 2:
                            sp.wait_ge(o_done, b * NT + i - 1)
                        sp.dma_start(xr[:, i % 2, :], seq[bass.ds(b, 1), :, i, :]).then_inc(xr_in[i % 2], 16)
                        if i >= 1:
                            sp.wait_ge(o_done, b * NT + i)
                            sp.dma_start(oseq[bass.ds(b, 1), :, i - 1, :], o[:, (i - 1) % 2, :]).then_inc(o_out[(i - 1) % 2], 16)
                    sp.wait_ge(o_done, b * NT + NT)
                    sp.dma_start(oseq[bass.ds(b, 1), :, NT - 1, :], o[:, (NT - 1) % 2, :]).then_inc(o_out[(NT - 1) % 2], 16)
                sp.wait_ge(xl_in, 16 * (B + 1))
                for r in range(2):
                    sp.wait_ge(o_out[r], 16 * B * NT // 2)

            @block.scalar
            def _(act):
                act.wait_ge(g_in, 32)
                nc.scalar.activation(gate[:, 2:3], gate[:, 0:1], ACT.Exp, scale=-1.0).then_inc(gexp, 1)
                nc.scalar.activation(gate[:, 4:5], gate[:, 1:2], ACT.Exp).then_inc(gexp, 1)
                with act.Fori(0, B) as b:
                    for i in range(8):
                        act.wait_ge(hT_ps, b * 8 + i + 1)
                        nc.scalar.activation(hT[:, i % 4, (i // 4) * 512:(i // 4) * 512 + 512], bank[i][:, :],
                                             ACT.Relu).then_inc(hT_done, 1)
                    for n in range(2 * NT):
                        act.wait_ge(z_ps, b * (2 * NT) + n + 1)
                        dst = (rows_l, rows_g)[n // NT][:, n % NT, :]
                        nc.scalar.activation(dst, bank[n % 8][:, :], ACT.Copy).then_inc(z_copied, 1)
                        nc.scalar.activation(bank[n % 8][:, :], bank[n % 8][:, :], ACT.Square,
                                             accum_out=ss[:, n // NT, n % NT:n % NT + 1]).then_inc(z_squared, 1)
                    for n in range(16):
                        act.wait_ge(zT_ps, b * 16 + n + 1)
                        nc.scalar.activation(zT[n // 8][:, n % 4, (n % 8 // 4) * 512:(n % 8 // 4) * 512 + 512],
                                             bank[4 + n % 4][:, :], ACT.Copy).then_inc(zT_done, 1)
                    for i in range(NT):
                        act.wait_ge(v_ps, b * NT + i + 1)
                        nc.scalar.activation(v[:, i, :], bank[i % 4][:, :], ACT.Copy).then_inc(v_done, 1)
                    for i in range(NT):
                        act.wait_ge(g_used, b * NT + i + 1)
                        nc.scalar.activation(A[1][:, :], A[1][:, :], ACT.Exp, scale=INV_S2).then_inc(exp_done, 1)
                        for q in range(2):
                            act.wait_ge(KT_ps, b * (2 * NT) + 2 * i + q + 1)
                            nc.scalar.activation(KT[:, q * 512:q * 512 + 512], bank[4 + q], ACT.Copy).then_inc(KT_done, 1)

            @block.vector
            def _(dve):
                nlink, base = [0], [0]

                def link(ins):
                    nlink[0] += 1
                    ins.then_inc(glink if base[0] is None else vlink, 1)
                    if base[0] is None:
                        dve.wait_ge(glink, nlink[0])
                    else:
                        dve.wait_ge(vlink, base[0] + nlink[0])

                base[0] = None
                dve.wait_ge(gexp, 2)
                link(nc.vector.tensor_scalar(gate[:, 2:3], gate[:, 2:3], 1.0, None, ALU.add))
                link(nc.vector.reciprocal(WL, gate[:, 2:3]))
                link(nc.vector.tensor_scalar(WG, WL, -1.0, 1.0, ALU.mult, ALU.add))
                link(nc.vector.tensor_tensor(gate[:, 4:5], gate[:, 4:5], gate[:, 4:5], ALU.mult))
                link(nc.vector.reciprocal(INV_S2, gate[:, 4:5]))
                for n in range(16):
                    dve.wait_ge(gw_ps, n + 1)
                    dst = (wT[0], wT[1], woT, wT[2])[n // 4][:, n % 4, :]
                    nc.vector.tensor_copy(dst, bank[n % 8][:, :]).then_inc(gw_done, 1)
                dve.wait_ge(adjm_in, 16)
                for i in range(NT):
                    dg = adj_m[:, i, i * P:(i + 1) * P]
                    nc.vector.tensor_tensor(dg, dg, off_diag[:, :], ALU.mult).then_inc(adjm_done, 1)
                with dve.Fori(0, B) as b:
                    nlink[0] = 0
                    base[0] = dve.snap(b * LINKS)
                    dve.wait_ge(xl_in, (b + 1) * 16)
                    for j in range(NT):
                        nc.vector.bn_stats(stats[:, j, :], xl[:, j, :]).then_inc(vlink, 1)
                    nlink[0] += NT
                    dve.wait_ge(vlink, base[0] + nlink[0])
                    nc.vector.memset(nrm[:, 2, :], 0.0)
                    for j in range(NT):
                        nc.vector.bn_aggr(mv[:, j, :], stats[:, j, :]).then_inc(vlink, 1)
                    nlink[0] += NT
                    dve.wait_ge(vlink, base[0] + nlink[0])
                    link(nc.vector.tensor_scalar(nrm[:, 0, :], mv[:, :, 1], LN_EPS, None, ALU.add))
                    rsqrt(nc.vector, link, nrm[:, 0, :], nrm[:, 1, :], nrm[:, 2, :])
                    for j in range(NT):
                        nc.vector.tensor_scalar(rows_l[:, j, :], xl[:, j, :], mv[:, j, 0:1], nrm[:, 1, j:j + 1],
                                                ALU.subtract, ALU.mult).then_inc(ln_done, 1)
                    dve.wait_ge(z_squared, b * (2 * NT) + 2 * NT)
                    link(nc.vector.tensor_scalar(nrm[:, 0, :], ss[:, 0, :], EPS * EPS, None, ALU.max))
                    rsqrt(nc.vector, link, nrm[:, 0, :], nrm[:, 1, :], nrm[:, 2, :])
                    for j in range(NT):
                        nc.vector.tensor_scalar(rows_l[:, j, :], rows_l[:, j, :], nrm[:, 1, j:j + 1], None,
                                                ALU.mult).then_inc(zn_done, 1)
                    link(nc.vector.tensor_scalar(ss[:, 1, :], ss[:, 1, :], -0.5, None, ALU.mult))
                    for j in range(NT):
                        nc.vector.tensor_scalar(K[:, j * P:(j + 1) * P], ident[:, :], ss[:, 1, j:j + 1], None,
                                                ALU.mult).then_inc(diag_done, 1)
                    for q in range(2):
                        dve.wait_ge(sq_ps, b * 2 + q + 1)
                        nc.vector.tensor_copy(half_sq[:, q * 512:q * 512 + 512], bank[4 + q][:, :]).then_inc(sq_done, 1)
                    dve.wait_ge(sq_done, b * 2 + 2)
                    dve.wait_ge(adjm_done, NT)
                    for i in range(NT):
                        dve.wait_ge(K_ready, b * NT + i)
                        dve.wait_ge(sim_l, b * NT + i + 1)
                        nc.vector.scalar_tensor_tensor(A[0][:, :], two_banks[0], 0.0, adj_m[:, i, :], ALU.max, ALU.mult,
                                                       accum_out=coef[:, 0:1]).then_inc(l_used, 1)
                        dve.wait_ge(sim_g, b * NT + i + 1)
                        nc.vector.scalar_tensor_tensor(A[1][:, :], two_banks[1], ss[:, 1, i:i + 1], half_sq[:, :],
                                                       ALU.add, ALU.add).then_inc(g_used, 1)
                        dve.wait_ge(exp_done, b * NT + i + 1)
                        dve.wait_ge(l_used, b * NT + i + 1)
                        link(nc.vector.scalar_tensor_tensor(A[1][:, :], A[1][:, :], 1.0, adj_m[:, i, :], ALU.min,
                                                            ALU.mult, accum_out=coef[:, 1:2]))
                        link(nc.vector.tensor_scalar(coef[:, :], coef[:, :], EPS, None, ALU.max))
                        link(nc.vector.reciprocal(coef[:, :], coef[:, :]))
                        link(nc.vector.tensor_tensor(coef[:, :], coef[:, :], gate[:, 2:4], ALU.mult))
                        link(nc.vector.tensor_scalar(A[0][:, :], A[0][:, :], coef[:, 0:1], None, ALU.mult))
                        dve.wait_ge(KT_done, b * (2 * NT) + 2 * i)
                        nc.vector.scalar_tensor_tensor(K[:, :], A[1][:, :], coef[:, 1:2], A[0][:, :],
                                                       ALU.mult, ALU.add).then_inc(K_ready, 1)
                        if i:
                            out_rows(dve, b, i - 1)
                    out_rows(dve, b, NT - 1)
                    assert nlink[0] == LINKS, nlink[0]

            @block.tensor
            def _(pe):
                def mm(dst, pairs):
                    for n, (l, r) in enumerate(pairs):
                        last = nc.tensor.matmul(dst, l, r, start=n == 0, stop=n == len(pairs) - 1)
                    return last

                pe.wait_ge(w_in, 64)
                for n in range(12):
                    if n >= 8:
                        pe.wait_ge(gw_done, n - 7)
                    src, k = raw[(0, 1, 3)[n // 4]], n % 4
                    for m in range(KD):
                        last = nc.tensor.transpose(bank[n % 8][:, m * P:(m + 1) * P], src[:, m, k * P:(k + 1) * P],
                                                   ident[:, :])
                    last.then_inc(gw_ps, 1)
                pe.wait_ge(gw_done, 12)
                for m in range(KD):
                    mm(bank[(12 + m) % 8][:, :], [(raw[2][:, k, m * P:(m + 1) * P], woT[:, k, :])
                                                  for k in range(KD)]).then_inc(gw_ps, 1)
                pe.wait_ge(gw_done, 16)
                with pe.Fori(0, B) as b:
                    pe.wait_ge(o_done, b * NT)
                    for i in range(8):
                        if i == 0:
                            pe.wait_ge(ln_done, b * NT + 4)
                        if i == 4:
                            pe.wait_ge(ln_done, b * NT + 8)
                        for j in range(4):
                            r = (i // 4) * 4 + j
                            last = nc.tensor.transpose(bank[i][:, j * P:(j + 1) * P],
                                                       rows_l[:, r, (i % 4) * P:(i % 4 + 1) * P], ident[:, :])
                        last.then_inc(hT_ps, 1)
                    pe.wait_ge(hT_done, b * 8 + 8)
                    for n in range(2 * NT):
                        if n >= 8:
                            pe.wait_ge(z_squared, b * (2 * NT) + n - 7)
                        mm(bank[n % 8][:, :], [(hT[:, k, (n % NT) * P:(n % NT + 1) * P], wT[n // NT][:, k, :])
                                               for k in range(KD)]).then_inc(z_ps, 1)
                    pe.wait_ge(z_squared, b * (2 * NT) + 2 * NT)
                    pe.wait_ge(diag_done, b * NT + NT)
                    for q in range(2):
                        for j in range(4):
                            last = nc.tensor.matmul(bank[4 + q][:, j * P:(j + 1) * P], ones[:, :],
                                                    K[:, (4 * q + j) * P:(4 * q + j + 1) * P],
                                                    start=j == 0, stop=True, skip_group_check=True)
                        last.then_inc(sq_ps, 1)
                    pe.wait_ge(sq_done, b * 2 + 2)
                    pe.wait_ge(zn_done, b * NT + NT)
                    for n in range(16):
                        if n >= 4:
                            pe.wait_ge(zT_done, b * 16 + n - 3)
                        for j in range(4):
                            r = (n % 8 // 4) * 4 + j
                            last = nc.tensor.transpose(bank[4 + n % 4][:, j * P:(j + 1) * P],
                                                       (rows_l, rows_g)[n // 8][:, r, (n % 4) * P:(n % 4 + 1) * P],
                                                       ident[:, :])
                        last.then_inc(zT_ps, 1)
                    pe.wait_ge(zT_done, b * 16 + 16)
                    for i in range(NT):
                        if i >= 4:
                            pe.wait_ge(v_done, b * NT + i - 3)
                        mm(bank[i % 4][:, :], [(hT[:, k, i * P:(i + 1) * P], wT[2][:, k, :])
                                               for k in range(KD)]).then_inc(v_ps, 1)
                    pe.wait_ge(v_done, b * NT + NT)

                    def sims(i):
                        for z, (ready, used) in enumerate(((sim_l, l_used), (sim_g, g_used))):
                            pe.wait_ge(used, b * NT + i)
                            for q in range(2):
                                last = mm(bank[2 * z + q], [(zT[z][:, k, i * P:(i + 1) * P],
                                                             zT[z][:, k, q * 512:q * 512 + 512]) for k in range(KD)])
                            last.then_inc(ready, 1)

                    def apply(i):
                        pe.wait_ge(K_ready, b * NT + i + 1)
                        for q in range(2):
                            for j in range(4):
                                last = nc.tensor.transpose(bank[4 + q][:, j * P:(j + 1) * P],
                                                           K[:, (4 * q + j) * P:(4 * q + j + 1) * P], ident[:, :])
                            last.then_inc(KT_ps, 1)
                        pe.wait_ge(KT_done, b * (2 * NT) + 2 * i + 2)
                        if i >= 2:
                            pe.wait_ge(o_done, b * NT + i - 1)
                        mm(bank[6 + i % 2], [(KT[:, j * P:(j + 1) * P], v[:, j, :])
                                             for j in range(NT)]).then_inc(o_ps, 1)

                    sims(0)
                    for i in range(NT):
                        if i + 1 < NT:
                            sims(i + 1)
                        apply(i)


_INS = ['x', 'adj', 'L0_gnn_b1', 'L0_gnn_W2', 'L0_gnn_b2', 'L1_gnn_W_lang', 'L1_gnn_W_grav', 'L1_gnn_W_V',
        'L1_gnn_W_O', 'L1_gnn_gate_logit', 'L1_gnn_log_sigma']


def kernel(**inputs):
    import numpy as np
    import concourse.bacc as bacc
    from concourse.bass_utils import run_bass_kernel_spmd

    nc = bacc.Bacc("TRN2", target_bir_lowering=False, num_devices=1)
    arrays, args = {}, []
    for name in _INS:
        a = np.ascontiguousarray(inputs[name])
        if a.ndim == 0:
            a = a.reshape(1)
        arrays[f"in_{name}"] = a
        args.append(nc.dram_tensor(f"in_{name}", a.shape, mybir.dt.from_np(a.dtype), kind="ExternalInput").ap())
    args.append(nc.dram_tensor("out", (B, T, D), F32, kind="ExternalOutput").ap())
    build(nc, *args)
    r = run_bass_kernel_spmd(nc, [arrays], core_ids=[0])
    return r.results[0]["out"]
```

```python
from contextlib import ExitStack

import concourse.bass as bass
import concourse.mybir as mybir
from concourse.alu_op_type import AluOpType as ALU

F32 = mybir.dt.float32
F16 = mybir.dt.float16
BF16 = mybir.dt.bfloat16
I32 = mybir.dt.int32
ACT = mybir.ActivationFunctionType
AX = mybir.AxisListType

P = 128
B, T, D = 8, 1024, 512
H = 2 * D
KD, KH = D // P, H // P
CH = 64
NCH = T // CH
JT = CH * B // P
STEPS_J = P // B
NT = T // P
PARTS = 3
SLOTS = PARTS + 1
LN_EPS = 1e-5
EPS = 1e-8
PART_PAIRS = ((0, 0), (0, 1), (1, 0))
START, DMA_START = 1, 16
EXP_MASK = 0x7F800000
RSQRT_SEED = float(0x5F3759DF)


def rsqrt_pieces(dve, link, settle, x, y, t):
    xi, yi = x.bitcast(I32), y.bitcast(I32)

    def seed():
        settle()
        link(dve.tensor_single_scalar(yi, xi, 1, ALU.logical_shift_right))
        link(dve.tensor_scalar(yi, yi, -1.0, RSQRT_SEED, ALU.mult, ALU.add), wait=False)

    def newton():
        settle()
        link(dve.scalar_tensor_tensor(t, y, -0.5, y, ALU.mult, ALU.mult))
        link(dve.tensor_tensor(t, t, x, ALU.mult))
        link(dve.scalar_tensor_tensor(y, t, 1.5, y, ALU.add, ALU.mult), wait=False)

    return [seed] + [newton] * 4


def rsqrt(dve, link, settle, x, y, t):
    for piece in rsqrt_pieces(dve, link, settle, x, y, t):
        piece()
    settle()


def build(nc, x, adj, b1, W2, b2, W_lang, W_grav, W_V, W_O, gate_logit, log_sigma, out):
    ctx = ExitStack()
    with ctx:
        x1 = nc.dram_tensor("x1", (B, T, D), F32, kind="Internal").ap()

        def sb(stack, name, shape, dt=F32):
            return stack.enter_context(nc.sbuf_tensor(name, shape, dt))

        def sem(name):
            return ctx.enter_context(nc.semaphore(name))

        psum = ctx.enter_context(nc.psum_tensor("psum", [P, 8, 512], F32))
        bank = [psum[:, i, :] for i in range(8)]
        ident = sb(ctx, "ident", [P, P])
        off_diag = sb(ctx, "off_diag", [P, P])
        ones = sb(ctx, "ones", [P, P])

        rec = ctx.enter_context(ExitStack())
        w1t = [sb(rec, f"w1t_{n}", [P, KD, H], F16) for n in ("hi", "lo")]
        w1m = [sb(rec, f"w1m_{n}", [P, KD, H], F16) for n in ("hi", "lo")]
        w2t = [sb(rec, f"w2t_{n}", [P, KH, D], F16) for n in ("hi", "lo")]
        b1c = sb(rec, "b1c", [P, KH])
        b2c = sb(rec, "b2c", [P, KD])
        scl = sb(rec, "scl", [P, 8])
        TWO_W = scl[:, 0:2]
        S1, S2 = scl[:, 2:3], scl[:, 3:4]
        INV_S12 = scl[:, 4:5]
        INV_S2 = scl[:, 5:6]
        HALF_INV_S2 = scl[:, 6:7]
        S12 = scl[:, 7:8]
        mem = sb(rec, "mem", [P, KD, B, PARTS])
        MEM_AT = (2, 0, 1)
        hid = sb(rec, "hid", [P, KH, PARTS, B])
        mem_hi = mem[:, :, :, :].rearrange("p k b s -> p (k b s)").bitcast(BF16).rearrange(
            "p (k b s two) -> p k s b two", b=B, s=PARTS, two=2)[:, :, :, :, 1]
        hid_hi = hid[:, :, :, :].rearrange("p k s b -> p (k s b)").bitcast(BF16).rearrange(
            "p (k s b two) -> p k s b two", b=B, s=PARTS, two=2)[:, :, :, :, 1]
        prod = sb(rec, "prod", [P, KD, B])
        pre_sum = sb(rec, "pre_sum", [P, KH, B])
        factors = sb(rec, "factors", [P, KD, B, PARTS])
        addends = sb(rec, "addends", [P, KD, B, PARTS])

        p_bank, y_bank = bank[0:2], bank[2:6]
        NG = 4
        GT = KH // NG
        y_ps = [b[:, 0:GT * SLOTS * B].rearrange("p (m s b) -> p m s b", s=SLOTS, b=B) for b in y_bank]
        y_slots = psum[:, 2:6, 0:GT * SLOTS * B].rearrange("p g (m s b) -> p g m s b", s=SLOTS, b=B)[:, :, :, PARTS, :]
        p_ps = [b[:, 0:KD // 2 * SLOTS * B].rearrange("p (m s b) -> p m s b", s=SLOTS, b=B) for b in p_bank]

        adj_in, w2_in, bias_in = sem("adj_in"), sem("w2_in"), sem("bias_in")
        const_set, const_ready = sem("const_set"), sem("const_ready")
        wmax_ready, wmax_all = sem("wmax_ready"), sem("wmax_all")
        wt_ps_ready, wt_hi_done, wt_done = sem("wt_ps_ready"), sem("wt_hi_done"), sem("wt_done")
        dve_link = sem("dve_link")

        with ExitStack() as tmp:
            adj_sb = sb(tmp, "adj_sb", [P, KH, H])
            w2_sb = sb(tmp, "w2_sb", [P, KD, H])
            wmax = sb(tmp, "wmax", [P, 2])
            jobs = ([("w1t", k, m) for k in range(KD) for m in (0, 4)]
                    + [("w1m", k, m) for k in range(KD) for m in (0, 4)]
                    + [("w2", k, 0) for k in range(KH)])
            block = tmp.enter_context(nc.Block())

            @block.sync
            def _(sp):
                sp.dma_start(adj_sb[:, :, :], adj.rearrange("(m p) k -> p m k", p=P)).then_inc(adj_in, 16)
                sp.dma_start(w2_sb[:, :, :], W2.rearrange("(m p) k -> p m k", p=P)).then_inc(w2_in, 16)
                with nc.allow_non_contiguous_dma(reason="1536 words, once"):
                    sp.dma_start(b1c[:, :], b1.rearrange("(m p) -> p m", p=P)).then_inc(bias_in, 16)
                    sp.dma_start(b2c[:, :], b2.rearrange("(m p) -> p m", p=P)).then_inc(bias_in, 16)

            @block.gpsimd
            def _(pool):
                pool.memset(ident[:, :], 0.0).then_inc(const_set, 1)
                pool.memset(ones[:, :], 1.0).then_inc(const_set, 1)
                pool.wait_ge(const_set, 2)
                pool.affine_select(ident[:, :], ident[:, :], [[-1, P]], ALU.not_equal, 1.0, base=0,
                                   channel_multiplier=1).then_inc(const_ready, 1)
                pool.affine_select(off_diag[:, :], ones[:, :], [[-1, P]], ALU.not_equal, 0.0, base=0,
                                   channel_multiplier=1).then_inc(const_ready, 1)
                pool.wait_ge(wmax_ready, 2)
                pool.partition_all_reduce(TWO_W, wmax[:, :], P, bass.bass_isa.ReduceOp.absmax).then_inc(wmax_all, 1)

            @block.tensor
            def _(pe):
                pe.wait_ge(const_ready, 2)
                pe.wait_ge(adj_in, 16)
                for n, (what, k, m) in enumerate(jobs):
                    if what == "w2" and k == 0:
                        pe.wait_ge(w2_in, 16)
                    if n >= 8:
                        pe.wait_ge(wt_done, n - 7)
                    for i in range(4):
                        src = w2_sb[:, i, k * P:(k + 1) * P] if what == "w2" else \
                            adj_sb[:, m + i, (k + KD * (what == "w1m")) * P:(k + 1 + KD * (what == "w1m")) * P]
                        last = nc.tensor.transpose(bank[n % 8][:, i * P:(i + 1) * P], src, ident[:, :])
                    last.then_inc(wt_ps_ready, 1)

            @block.vector
            def _(dve):
                n_link = [0]

                def link(ins):
                    n_link[0] += 1
                    ins.then_inc(dve_link, 1)
                    dve.wait_ge(dve_link, n_link[0])

                dve.wait_ge(adj_in, 16)
                nc.vector.tensor_reduce(wmax[:, 0:1], adj_sb[:, :, :], AX.XY, ALU.max,
                                        apply_absolute_value=True).then_inc(wmax_ready, 1)
                dve.wait_ge(w2_in, 16)
                nc.vector.tensor_reduce(wmax[:, 1:2], w2_sb[:, :, :], AX.XY, ALU.max,
                                        apply_absolute_value=True).then_inc(wmax_ready, 1)
                dve.wait_ge(wmax_all, 1)
                e = TWO_W.bitcast(I32)
                s = scl[:, 2:4].bitcast(I32)
                inv = scl[:, 4:6]
                link(nc.vector.tensor_single_scalar(e, e, EXP_MASK, ALU.bitwise_and))
                link(nc.vector.tensor_scalar(e, e, float(87 << 23), None, ALU.max))
                link(nc.vector.tensor_scalar(s, e, -1.0, float(268 << 23), ALU.mult, ALU.add))
                link(nc.vector.tensor_scalar(inv.bitcast(I32), e, float(-(14 << 23)), None, ALU.add))
                link(nc.vector.tensor_tensor(INV_S12, INV_S12, INV_S2, ALU.mult))
                link(nc.vector.tensor_scalar(HALF_INV_S2, INV_S2, 0.5, None, ALU.mult))
                link(nc.vector.tensor_tensor(S12, S1, S2, ALU.mult))
                dve.wait_ge(bias_in, 32)
                link(nc.vector.tensor_scalar(b1c[:, :], b1c[:, :], S12, None, ALU.mult))
                link(nc.vector.memset(mem[:, :, :, :], 0.0))
                link(nc.vector.memset(factors[:, :, :, :], 0.0))
                link(nc.vector.memset(factors[:, :, :, 2], 0.5))
                link(nc.vector.memset(addends[:, :, :, :], 0.0))
                for n, (what, k, m) in enumerate(jobs):
                    dve.wait_ge(wt_ps_ready, n + 1)
                    src = bank[n % 8][:, :]
                    parts, at, s = {"w1t": (w1t, m * P, S1), "w1m": (w1m, m * P, S1), "w2": (w2t, 0, S2)}[what]
                    hi, lo = (w[:, k, at:at + 512] for w in parts)
                    nc.vector.tensor_scalar(hi, src, s, None, ALU.mult).then_inc(wt_hi_done, 1)
                    dve.wait_ge(wt_hi_done, n + 1)
                    nc.vector.scalar_tensor_tensor(lo, src, s, hi, ALU.mult, ALU.subtract).then_inc(wt_done, 1)

        with ExitStack() as tmp:
            xa = sb(tmp, "xa", [P, JT, D])
            xc = sb(tmp, "xc", [P, JT, D])
            xn = sb(tmp, "xn", [P, JT, D])
            tok = [sb(tmp, f"tok_{n}", [P, KD, CH * B], F16) for n in ("hi", "lo")]
            pre = sb(tmp, "pre", [P, 2, KH, (CH + 1) * B])
            hist = sb(tmp, "hist", [P, KD, CH * B])
            xo = sb(tmp, "xo", [P, JT, D])
            stats = sb(tmp, "stats", [P, JT, 6])
            mv = sb(tmp, "mv", [P, JT, 2])
            nrm = sb(tmp, "nrm", [P, 3, JT])
            table = sb(tmp, "table", [P, 1])

            x_in, xc_in, x1_out = sem("x_in"), sem("xc_in"), sem("x1_out")
            x_used, tok_ps_ready = sem("x_used"), sem("tok_ps_ready")
            tok_hi_ready, tok_ready = sem("tok_hi_ready"), sem("tok_ready")
            pre_ps_ready, pre_ready, slot_ready = sem("pre_ps_ready"), sem("pre_ready"), sem("slot_ready")
            rows_ps_ready, xo_ready = sem("rows_ps_ready"), sem("xo_ready")
            chain = sem("chain")
            y_ready = [sem(f"y_ready_{g}") for g in range(NG)]
            ysum_ready = [sem(f"ysum_ready_{g}") for g in range(NG)]
            gelu_ready = [sem(f"gelu_ready_{g}") for g in range(NG)]
            hid_r1 = [sem(f"hid_r1_{g}") for g in range(NG)]
            hid_ready = [sem(f"hid_ready_{g}") for g in range(NG)]
            fill_ready, fill_done = sem("fill_ready"), sem("fill_done")
            p_ready = [sem("p_ready_a"), sem("p_ready_b")]
            psum_read = [sem("psum_read_a"), sem("psum_read_b")]
            diff_ready = [sem("diff_ready_a"), sem("diff_ready_b")]
            tanh_ready = [sem("tanh_ready_a"), sem("tanh_ready_b")]
            mem_new = [sem("mem_new_a"), sem("mem_new_b")]
            mem_r1 = [sem("mem_r1_a"), sem("mem_r1_b")]
            mem_ready = [sem("mem_ready_a"), sem("mem_ready_b")]
            slots_written = sem("slots_written")
            hist_done, mem_added = sem("hist_done"), sem("mem_added")
            bias_slot = sem("bias_slot")

            FK = KD
            FW = CH * B // 2
            FPIECE = FW // FK
            FILLS = 2 * KH
            PRE_T = (CH + 1) * B
            pre_pieces = pre[:, :, :, :].rearrange("p a m t -> p (a m t)")
            psum_flat = psum[:, :, :].rearrange("p a c -> p (a c)")

            def rows(t, c, j):
                return t[:, bass.ds(c * CH + j * STEPS_J, STEPS_J), :].rearrange("b t d -> t b d")

            block = tmp.enter_context(nc.Block())

            @block.sync
            def _(sp):
                for first in range(2):
                    sp.wait_ge(x_used, first * JT)
                    for j in range(JT):
                        sp.dma_start(xa[:, j, :], rows(x, first, j)).then_inc(x_in, 16)
                with sp.Fori(0, NCH) as c:
                    sp.wait_ge(xo_ready, c * JT + START)
                    for j in range(JT):
                        sp.dma_start(xc[:, j, :], rows(x, c, j)).then_inc(xc_in, 16)
                    nxt = sp.snap((c + 2) % NCH)
                    sp.wait_ge(x_used, (c + 2) * JT)
                    for j in range(JT):
                        sp.dma_start(xa[:, j, :], rows(x, nxt, j)).then_inc(x_in, 16)
                    for j in range(JT):
                        sp.wait_ge(xo_ready, c * JT + (j + 1 + START))
                        sp.dma_start(rows(x1, c, j), xo[:, j, :]).then_inc(x1_out, 16)
                sp.wait_ge(x_in, 16 * JT * (NCH + 2))
                sp.wait_ge(x1_out, 16 * JT * NCH + DMA_START)

            @block.gpsimd
            def _(pool):
                pool.sem_inc(hist_done, START)
                with pool.Fori(0, NCH) as c:
                    with pool.Fori(0, CH) as t:
                        now = pool.snap(c * CH + t + 1)
                        pool.wait_ge(mem_new[0], now)
                        pool.wait_ge(mem_new[1], now)
                        pool.tensor_copy(hist[:, :, bass.ds(t * B, B)], mem[:, :, :, 2]).then_inc(hist_done, 1)

            @block.scalar
            def _(act):
                half_inv_s2, inv_s12, s2 = (act.alloc_register(n) for n in ("half_inv_s2", "inv_s12", "s2"))
                act.sem_inc(fill_done, START)
                nc.scalar.activation(table[:, :], mem[:, 0, 0, 0:1], ACT.Gelu)
                act.reg_load(half_inv_s2, HALF_INV_S2[0:1, :].bitcast(I32))
                act.reg_load(inv_s12, INV_S12[0:1, :].bitcast(I32))
                act.reg_load(s2, S2[0:1, :].bitcast(I32))

                def take_tokens(n):
                    for k in range(KD):
                        act.wait_ge(tok_ps_ready, n * KD + k + 1)
                        nc.scalar.activation(tok[0][:, k, :], bank[2 + k][:, :], ACT.Relu).then_inc(tok_hi_ready, 1)

                take_tokens(0)
                act.wait_ge(fill_ready, 1)
                take_tokens(1)
                act.wait_ge(pre_ready, KH)
                with act.Fori(0, NCH) as c:
                    now_pre = pre[:, bass.ds(c % 2, 1), :, :].rearrange("p a (g m) t -> p (a g) m t", g=NG)
                    act.wait_ge(tok_ready, (c + 2) * KD)
                    act.wait_ge(xo_ready, c * JT + START)
                    act.wait_ge(fill_done, c * CH + START)
                    nc.scalar.activation(y_slots, now_pre[:, :, :, 0:B], ACT.Copy).then_inc(slots_written, 1)
                    with act.Fori(0, CH) as t:
                        now = act.snap(c * CH + t + 1)
                        for g in range(NG):
                            act.wait_ge(ysum_ready[g], now)
                            nc.scalar.activation(hid[:, GT * g:GT * g + GT, 0, :], pre_sum[:, GT * g:GT * g + GT, :],
                                                 ACT.Gelu, scale=inv_s12).then_inc(gelu_ready[g], 1)
                        act.wait_ge(fill_done, c * CH + (t + START))
                        nc.scalar.activation(y_slots, now_pre[:, :, :, bass.ds((t + 1) * B, B)],
                                             ACT.Copy).then_inc(slots_written, 1)
                        g = act.snap(c * CH + t + CH - FK)
                        q = act.snap(g % CH)
                        act.wait_ge(fill_ready, (c * CH + t) // FK + 1)
                        nc.scalar.activation(
                            pre_pieces[:, bass.ds((g // CH) % 2 * (KH * PRE_T) + q // (CH // KH) * PRE_T
                                                  + q % (CH // KH) * FPIECE, FPIECE)],
                            psum_flat[:, bass.ds(6 * 512 + q // FK % 2 * 512 + q % FK * FPIECE, FPIECE)],
                            ACT.Identity, bias=b1c[:, bass.ds(q // (CH // KH), 1)], scale=s2).then_inc(fill_done, 1)
                        for h in range(2):
                            act.wait_ge(psum_read[h], now)
                            nc.scalar.activation(factors[:, 2 * h:2 * h + 2, :, 1], prod[:, 2 * h:2 * h + 2, :],
                                                 ACT.Tanh, scale=half_inv_s2).then_inc(tanh_ready[h], 1)
                    act.wait_ge(fill_ready, (c + 1) * FILLS + 1)
                    take_tokens(c + 2)

            def sum_products(dve, h, now):
                dve.wait_ge(p_ready[h], now)
                nc.vector.tensor_reduce(prod[:, 2 * h:2 * h + 2, :], p_ps[h].rearrange("p m s b -> p m b s"),
                                        AX.X, ALU.add).then_inc(psum_read[h], 1)

            def update(dve, h, now):
                k = slice(2 * h, 2 * h + 2)
                dve.wait_ge(tanh_ready[h], now)
                dve.wait_ge(diff_ready[h], now)
                nc.vector.tensor_tensor_scan(flat(mem, k), flat(factors, k), flat(addends, k), 0.0,
                                             ALU.mult, ALU.add).then_inc(mem_new[h], 1)

            def difference(dve, h, now):
                k = slice(2 * h, 2 * h + 2)
                dve.wait_ge(psum_read[h], now)
                nc.vector.tensor_tensor(addends[:, k, :, 0:2],
                                        prod[:, k, :].unsqueeze(3).to_broadcast([P, 2, B, 2]),
                                        mem[:, k, :, MEM_AT[0]].unsqueeze(3).to_broadcast([P, 2, B, 2]),
                                        ALU.subtract).then_inc(diff_ready[h], 1)

            def flat(t, k):
                return t[:, k, :, :].rearrange("p k b s -> p (k b s)")

            def first_rest(dve, h, now):
                k = slice(2 * h, 2 * h + 2)
                dve.wait_ge(mem_new[h], now)
                nc.vector.tensor_tensor(mem[:, k, :, MEM_AT[1]], mem[:, k, :, MEM_AT[0]],
                                        mem_hi[:, k, MEM_AT[0], :], ALU.subtract).then_inc(mem_r1[h], 1)

            def second_rest(dve, h, now):
                k = slice(2 * h, 2 * h + 2)
                dve.wait_ge(mem_r1[h], now)
                nc.vector.tensor_tensor(mem[:, k, :, MEM_AT[2]], mem[:, k, :, MEM_AT[1]],
                                        mem_hi[:, k, MEM_AT[1], :], ALU.subtract).then_inc(mem_ready[h], 1)

            @block.vector
            def _(dve):
                nlink = [0]
                at = [None]

                def settle():
                    dve.wait_ge(chain, at[0] + nlink[0])

                def link(ins, wait=True):
                    nlink[0] += 1
                    ins.then_inc(chain, 1)
                    if wait:
                        settle()

                dve.sem_inc(mem_ready[0], START)
                dve.sem_inc(mem_ready[1], START)
                dve.sem_inc(xo_ready, START)
                dve.sem_inc(mem_added, START)
                dve.sem_inc(x1_out, DMA_START)
                dve.wait_ge(bias_in, 32)
                for k in range(KD):
                    nc.vector.tensor_scalar(p_ps[k // 2][:, k % 2, PARTS, :],
                                            ones[:, 0:B], b2c[:, k:k + 1], S2, ALU.mult,
                                            ALU.mult).then_inc(bias_slot, 1)
                nc.vector.memset(pre[:, :, :, CH * B:], 0.0).then_inc(bias_slot, 1)
                PER_CHUNK = 2 * JT + 15

                def norm_pieces(n):
                    base = n * PER_CHUNK if isinstance(n, int) else dve.snap(n * PER_CHUNK)
                    var, y, t = nrm[:, 0, :], nrm[:, 1, :], nrm[:, 2, :]

                    def start():
                        nlink[0] = 0
                        at[0] = base
                        dve.wait_ge(x_in, (n + 1) * (16 * JT))

                    def row_stats(j):
                        nc.vector.bn_stats(stats[:, j, :], xa[:, j, :]).then_inc(chain, 1)
                        nlink[0] += 1

                    def spread():
                        dve.wait_ge(chain, at[0] + nlink[0])
                        nc.vector.memset(nrm[:, 2, :], 0.0)
                        for j in range(JT):
                            nc.vector.bn_aggr(mv[:, j, :], stats[:, j, :]).then_inc(chain, 1)
                        nlink[0] += JT
                        dve.wait_ge(chain, at[0] + nlink[0])
                        link(nc.vector.tensor_scalar(var, mv[:, :, 1], LN_EPS, None, ALU.add), wait=False)

                    def scaled(j):
                        if j == 0:
                            assert nlink[0] == PER_CHUNK
                            settle()
                            dve.wait_ge(tok_ps_ready, n * KD)
                        nc.vector.tensor_scalar(xn[:, j, :], xa[:, j, :], mv[:, j, 0:1], y[:, j:j + 1],
                                                ALU.subtract, ALU.mult).then_inc(x_used, 1)

                    def first_stats():
                        start()
                        row_stats(0)

                    return ([first_stats] + [lambda j=j: row_stats(j) for j in range(1, JT)] + [spread]
                            + rsqrt_pieces(nc.vector, link, settle, var, y, t)
                            + [lambda j=j: scaled(j) for j in range(JT)])

                def layer_norm(n):
                    for piece in norm_pieces(n):
                        piece()

                def split_tokens(n):
                    for k in range(KD):
                        dve.wait_ge(tok_hi_ready, n * KD + (k + 1))
                        nc.vector.scalar_tensor_tensor(tok[1][:, k, :], bank[2 + k][:, :], 0.0, tok[0][:, k, :],
                                                       ALU.max, ALU.subtract).then_inc(tok_ready, 1)

                layer_norm(0)
                split_tokens(0)
                for m in range(KH):
                    dve.wait_ge(pre_ps_ready, m + 1)
                    nc.vector.tensor_scalar(pre[:, 0, m, 0:CH * B], bank[2 + m % 4], S2, b1c[:, m:m + 1],
                                            ALU.mult, ALU.add).then_inc(pre_ready, 1)
                layer_norm(1)
                split_tokens(1)

                def step(now):
                    def take_sum(g):
                        dve.wait_ge(y_ready[g], now)
                        nc.vector.tensor_reduce(pre_sum[:, GT * g:GT * g + GT, :],
                                                y_ps[g].rearrange("p m s b -> p m b s"),
                                                AX.X, ALU.add).then_inc(ysum_ready[g], 1)

                    def hid_rest(g, i):
                        dve.wait_ge((gelu_ready, hid_r1)[i][g], now)
                        k = slice(GT * g, GT * g + GT)
                        nc.vector.tensor_tensor(hid[:, k, i + 1, :], hid[:, k, i, :], hid_hi[:, k, i, :],
                                                ALU.subtract).then_inc((hid_r1, hid_ready)[i][g], 1)

                    take_sum(0)
                    take_sum(1)
                    take_sum(2)
                    hid_rest(0, 0)
                    take_sum(3)
                    hid_rest(0, 1)
                    hid_rest(1, 0)
                    hid_rest(2, 0)
                    hid_rest(1, 1)
                    hid_rest(2, 1)
                    hid_rest(3, 0)
                    hid_rest(3, 1)
                    sum_products(dve, 0, now)
                    dve.wait_ge(mem_added, now)
                    difference(dve, 0, now)
                    dve.wait_ge(hist_done, now)
                    update(dve, 0, now)
                    first_rest(dve, 0, now)
                    sum_products(dve, 1, now)
                    second_rest(dve, 0, now)
                    difference(dve, 1, now)
                    update(dve, 1, now)
                    first_rest(dve, 1, now)
                    second_rest(dve, 1, now)
                    dve.wait_ge(mem_new[1], now)
                    nc.vector.tensor_copy(addends[:, :, :, 2], mem[:, :, :, MEM_AT[0]]).then_inc(mem_added, 1)

                with dve.Fori(0, NCH) as c:
                    pieces = norm_pieces(c + 2)
                    per = CH // (len(pieces) + 1)
                    for n, piece in enumerate(pieces):
                        with dve.Fori(0, per) as t:
                            step(dve.snap(c * CH + (t + (n * per + 1))))
                        piece()
                    with dve.Fori(len(pieces) * per, CH) as t:
                        step(dve.snap(c * CH + t + 1))
                    split_tokens(c + 2)
                    dve.wait_ge(xc_in, (c + 1) * (16 * JT))
                    dve.wait_ge(x1_out, c * (16 * JT) + DMA_START)
                    for j in range(JT):
                        dve.wait_ge(rows_ps_ready, c * JT + j + 1)
                        nc.vector.scalar_tensor_tensor(xo[:, j, :], bank[2 + j][:, :], INV_S2, xc[:, j, :],
                                                       ALU.mult, ALU.add).then_inc(xo_ready, 1)

            @block.tensor
            def _(pe):
                W = PARTS * B

                def product(banks, m, per, w, parts, k, first):
                    at = (m % per) * SLOTS * B
                    for i in range(2):
                        last = nc.tensor.matmul(banks[m // per][:, at:at + W], w[i][:, k, m * P:(m + 1) * P],
                                                parts[:, k, :, :], start=first and m % per == 0 and i == 0,
                                                stop=True, skip_group_check=True)
                    return last

                def give_tokens(n):
                    pe.wait_ge(x_used, (n + 1) * JT)
                    for k in range(KD):
                        for j in range(JT):
                            last = nc.tensor.transpose(bank[2 + k][:, j * P:(j + 1) * P],
                                                       xn[:, j, k * P:(k + 1) * P], ident[:, :])
                        last.then_inc(tok_ps_ready, 1)

                def fill(t, piece):
                    m, half, k = t // FK // 2, t // FK % 2, t % FK
                    at = piece * (FW // 2)
                    for n, (w, x) in enumerate(PART_PAIRS):
                        last = nc.tensor.matmul(bank[6 + half][:, at:at + FW // 2], w1t[w][:, k, m * P:(m + 1) * P],
                                                tok[x][:, k, half * FW + at:half * FW + at + FW // 2],
                                                start=k == 0 and piece == 0 and n == 0, stop=True,
                                                skip_group_check=True)
                    if k == FK - 1 and piece == 1:
                        last.then_inc(fill_ready, 1)

                def step(c, t):
                    now = pe.snap(c * CH + (t + 1))
                    pe.wait_ge(slots_written, c * (CH + 1) + (t + 1))
                    pe.wait_ge(mem_ready[0], now)
                    for m in range(KH):
                        for k in (0, 1):
                            product(y_bank, m, GT, w1m, mem_hi, k, k == 0)
                    pe.wait_ge(mem_ready[1], now)
                    for m in range(KH):
                        for k in (2, 3):
                            last = product(y_bank, m, GT, w1m, mem_hi, k, False)
                        if m % GT == GT - 1:
                            last.then_inc(y_ready[m // GT], 1)
                    fill(t, 0)
                    for h in range(2):
                        for q in range(NG):
                            if h == 0:
                                pe.wait_ge(hid_ready[q], now)
                            for m in range(2 * h, 2 * h + 2):
                                for k in range(GT * q, GT * q + GT):
                                    last = product(p_bank, m, 2, w2t, hid_hi, k, k == 0)
                        last.then_inc(p_ready[h], 1)
                    fill(t, 1)

                give_tokens(0)
                pe.wait_ge(tok_ready, KD)
                for m in range(KH):
                    if m >= 4:
                        pe.wait_ge(pre_ready, m - 3)
                    for k in range(KD):
                        for n, (w, x) in enumerate(PART_PAIRS):
                            last = nc.tensor.matmul(bank[2 + m % 4][:, :], w1t[w][:, k, m * P:(m + 1) * P],
                                                    tok[x][:, k, :], start=k == 0 and n == 0,
                                                    stop=k == KD - 1 and n == len(PART_PAIRS) - 1)
                    last.then_inc(pre_ps_ready, 1)
                pe.wait_ge(bias_slot, KD + 1)
                pe.wait_ge(pre_ready, KH)
                for t in range(CH - FK, CH):
                    for piece in range(2):
                        fill(t, piece)
                give_tokens(1)
                with pe.Fori(0, NCH) as c:
                    for t in range(CH):
                        step(c, t)
                    for g in range(NG):
                        pe.wait_ge(ysum_ready[g], (c + 1) * CH)
                    pe.wait_ge(slots_written, (c + 1) * (CH + 1))
                    give_tokens(c + 2)
                    pe.wait_ge(hist_done, (c + 1) * CH + START)
                    for j in range(JT):
                        pe.wait_ge(tok_ready, c * KD + (2 * KD + j + 1))
                        for k in range(KD):
                            last = nc.tensor.transpose(bank[2 + j][:, k * P:(k + 1) * P],
                                                       hist[:, k, j * P:(j + 1) * P], ident[:, :])
                        last.then_inc(rows_ps_ready, 1)

        rec.close()
        with ExitStack() as tmp:
            xl = sb(tmp, "xl", [P, NT, D])
            rows_l = sb(tmp, "rows_l", [P, NT, D])
            rows_g = sb(tmp, "rows_g", [P, NT, D])
            hT = sb(tmp, "hT", [P, KD, T])
            zT = [sb(tmp, f"zT_{n}", [P, KD, T]) for n in "lg"]
            v = rows_l
            wT = [sb(tmp, f"wT_{n}", [P, KD, D]) for n in ("lang", "grav", "vo")]
            half_sq = sb(tmp, "half_sq", [P, T])
            A = [sb(tmp, f"A_{n}", [P, T]) for n in "lg"]
            K = sb(tmp, "K", [P, T])
            KT = sb(tmp, "KT", [P, T])
            xr = sb(tmp, "xr", [P, 2, D])
            o = sb(tmp, "o", [P, 2, D])
            stats = sb(tmp, "g_stats", [P, NT, 6])
            mv = sb(tmp, "g_mv", [P, NT, 2])
            nrm = sb(tmp, "g_nrm", [P, 3, NT])
            ss = sb(tmp, "ss", [P, 2, NT])
            adj_m = sb(tmp, "adj_m", [P, NT, T])
            coef = sb(tmp, "coef", [P, 2])
            gate = sb(tmp, "gate", [P, 8])
            WL, WG, INV_S2 = gate[:, 2:3], gate[:, 3:4], gate[:, 4:5]
            raw = [rows_l[:, 0:4, :], rows_l[:, 4:8, :], rows_g[:, 0:4, :], rows_g[:, 4:8, :]]
            woT = zT[0][:, :, 0:D]

            w_in, g_in = sem("w_in"), sem("g_in")
            gw_ps, gw_done = sem("gw_ps"), sem("gw_done")
            gexp, glink = sem("gexp"), sem("glink")
            xl_in, xr_in, o_out = sem("xl_in"), (sem("xr_in_0"), sem("xr_in_1")), (sem("o_out_0"), sem("o_out_1"))
            ln_done, hT_ps, hT_done = sem("ln_done"), sem("hT_ps"), sem("hT_done")
            z_ps = sem("z_ps")
            z_copied, z_squared = sem("z_copied"), sem("z_squared")
            zn_done, diag_done, sq_ps, sq_done = sem("zn_done"), sem("diag_done"), sem("sq_ps"), sem("sq_done")
            v_ps, v_done = sem("v_ps"), sem("v_done")
            zT_ps, zT_done = sem("zT_ps"), sem("zT_done")
            sim_l, sim_g, l_used, g_used = sem("sim_l"), sem("sim_g"), sem("l_used"), sem("g_used")
            exp_done = sem("exp_done")
            K_ready, KT_ps, KT_done = sem("K_ready"), sem("KT_ps"), sem("KT_done")
            o_ps, o_done = sem("o_ps"), sem("o_done")
            vlink, adjm_in, adjm_done = sem("vlink"), sem("adjm_in"), sem("adjm_done")
            LINKS = 47 + 5 * NT

            def out_rows(dve, b, i):
                dve.wait_ge(o_ps, b * NT + i + 1)
                dve.wait_ge(xr_in[i % 2], (b * (NT // 2) + i // 2 + 1) * 16)
                dve.wait_ge(o_out[i % 2], (b * (NT // 2) + i // 2) * 16)
                nc.vector.tensor_tensor(o[:, i % 2, :], bank[6 + i % 2][:, :], xr[:, i % 2, :], ALU.add).then_inc(o_done, 1)

            two_banks = [psum[:, 2 * z:2 * z + 2, :].rearrange("p a c -> p (a c)") for z in range(2)]

            block = tmp.enter_context(nc.Block())

            @block.sync
            def _(sp):
                for n, w in enumerate((W_lang, W_grav, W_V, W_O)):
                    sp.dma_start(raw[n], w.rearrange("(m p) k -> p m k", p=P)).then_inc(w_in, 16)
                sp.dma_start(adj_m[:, :, :], adj.rearrange("(m p) k -> p m k", p=P)).then_inc(adjm_in, 16)
                sp.dma_start(gate[:, 0:1], gate_logit.partition_broadcast(P)).then_inc(g_in, 16)
                sp.dma_start(gate[:, 1:2], log_sigma.partition_broadcast(P)).then_inc(g_in, 16)
                seq = x1.rearrange("b (n p) d -> b p n d", p=P)
                oseq = out.rearrange("b (n p) d -> b p n d", p=P)
                sp.dma_start(xl[:, :, :], seq[0]).then_inc(xl_in, 16)
                with sp.Fori(0, B) as b:
                    nxt = sp.snap((b + 1) % B)
                    sp.wait_ge(ln_done, (b + 1) * NT)
                    sp.dma_start(xl[:, :, :], seq[bass.ds(nxt, 1), :, :, :]).then_inc(xl_in, 16)
                    for i in range(NT):
                        if i >= 2:
                            sp.wait_ge(o_done, b * NT + i - 1)
                        sp.dma_start(xr[:, i % 2, :], seq[bass.ds(b, 1), :, i, :]).then_inc(xr_in[i % 2], 16)
                        if i >= 1:
                            sp.wait_ge(o_done, b * NT + i)
                            sp.dma_start(oseq[bass.ds(b, 1), :, i - 1, :], o[:, (i - 1) % 2, :]).then_inc(o_out[(i - 1) % 2], 16)
                    sp.wait_ge(o_done, b * NT + NT)
                    sp.dma_start(oseq[bass.ds(b, 1), :, NT - 1, :], o[:, (NT - 1) % 2, :]).then_inc(o_out[(NT - 1) % 2], 16)
                sp.wait_ge(xl_in, 16 * (B + 1))
                for r in range(2):
                    sp.wait_ge(o_out[r], 16 * B * NT // 2)

            @block.scalar
            def _(act):
                act.wait_ge(g_in, 32)
                nc.scalar.activation(gate[:, 2:3], gate[:, 0:1], ACT.Exp, scale=-1.0).then_inc(gexp, 1)
                nc.scalar.activation(gate[:, 4:5], gate[:, 1:2], ACT.Exp).then_inc(gexp, 1)
                with act.Fori(0, B) as b:
                    for i in range(8):
                        act.wait_ge(hT_ps, b * 8 + i + 1)
                        nc.scalar.activation(hT[:, i % 4, (i // 4) * 512:(i // 4) * 512 + 512], bank[i][:, :],
                                             ACT.Relu).then_inc(hT_done, 1)
                    for n in range(2 * NT):
                        act.wait_ge(z_ps, b * (2 * NT) + n + 1)
                        dst = (rows_l, rows_g)[n // NT][:, n % NT, :]
                        nc.scalar.activation(dst, bank[n % 8][:, :], ACT.Copy).then_inc(z_copied, 1)
                        nc.scalar.activation(bank[n % 8][:, :], bank[n % 8][:, :], ACT.Square,
                                             accum_out=ss[:, n // NT, n % NT:n % NT + 1]).then_inc(z_squared, 1)
                    for n in range(16):
                        act.wait_ge(zT_ps, b * 16 + n + 1)
                        nc.scalar.activation(zT[n // 8][:, n % 4, (n % 8 // 4) * 512:(n % 8 // 4) * 512 + 512],
                                             bank[4 + n % 4][:, :], ACT.Copy).then_inc(zT_done, 1)
                    for i in range(NT):
                        act.wait_ge(v_ps, b * NT + i + 1)
                        nc.scalar.activation(v[:, i, :], bank[i % 4][:, :], ACT.Copy).then_inc(v_done, 1)
                    for i in range(NT):
                        act.wait_ge(g_used, b * NT + i + 1)
                        nc.scalar.activation(A[1][:, :], A[1][:, :], ACT.Exp, scale=INV_S2).then_inc(exp_done, 1)
                        for q in range(2):
                            act.wait_ge(KT_ps, b * (2 * NT) + 2 * i + q + 1)
                            nc.scalar.activation(KT[:, q * 512:q * 512 + 512], bank[4 + q], ACT.Copy).then_inc(KT_done, 1)

            @block.vector
            def _(dve):
                nlink, base = [0], [0]

                def settle():
                    if base[0] is None:
                        dve.wait_ge(glink, nlink[0])
                    else:
                        dve.wait_ge(vlink, base[0] + nlink[0])

                def link(ins, wait=True):
                    nlink[0] += 1
                    ins.then_inc(glink if base[0] is None else vlink, 1)
                    if wait:
                        settle()

                base[0] = None
                dve.wait_ge(gexp, 2)
                link(nc.vector.tensor_scalar(gate[:, 2:3], gate[:, 2:3], 1.0, None, ALU.add))
                link(nc.vector.reciprocal(WL, gate[:, 2:3]))
                link(nc.vector.tensor_scalar(WG, WL, -1.0, 1.0, ALU.mult, ALU.add))
                link(nc.vector.tensor_tensor(gate[:, 4:5], gate[:, 4:5], gate[:, 4:5], ALU.mult))
                link(nc.vector.reciprocal(INV_S2, gate[:, 4:5]))
                for n in range(16):
                    dve.wait_ge(gw_ps, n + 1)
                    dst = (wT[0], wT[1], woT, wT[2])[n // 4][:, n % 4, :]
                    nc.vector.tensor_copy(dst, bank[n % 8][:, :]).then_inc(gw_done, 1)
                dve.wait_ge(adjm_in, 16)
                for i in range(NT):
                    dg = adj_m[:, i, i * P:(i + 1) * P]
                    nc.vector.tensor_tensor(dg, dg, off_diag[:, :], ALU.mult).then_inc(adjm_done, 1)
                with dve.Fori(0, B) as b:
                    nlink[0] = 0
                    base[0] = dve.snap(b * LINKS)
                    dve.wait_ge(xl_in, (b + 1) * 16)
                    for j in range(NT):
                        nc.vector.bn_stats(stats[:, j, :], xl[:, j, :]).then_inc(vlink, 1)
                    nlink[0] += NT
                    dve.wait_ge(vlink, base[0] + nlink[0])
                    nc.vector.memset(nrm[:, 2, :], 0.0)
                    for j in range(NT):
                        nc.vector.bn_aggr(mv[:, j, :], stats[:, j, :]).then_inc(vlink, 1)
                    nlink[0] += NT
                    dve.wait_ge(vlink, base[0] + nlink[0])
                    link(nc.vector.tensor_scalar(nrm[:, 0, :], mv[:, :, 1], LN_EPS, None, ALU.add))
                    rsqrt(nc.vector, link, settle, nrm[:, 0, :], nrm[:, 1, :], nrm[:, 2, :])
                    for j in range(NT):
                        nc.vector.tensor_scalar(rows_l[:, j, :], xl[:, j, :], mv[:, j, 0:1], nrm[:, 1, j:j + 1],
                                                ALU.subtract, ALU.mult).then_inc(ln_done, 1)
                    dve.wait_ge(z_squared, b * (2 * NT) + 2 * NT)
                    link(nc.vector.tensor_scalar(nrm[:, 0, :], ss[:, 0, :], EPS * EPS, None, ALU.max))
                    rsqrt(nc.vector, link, settle, nrm[:, 0, :], nrm[:, 1, :], nrm[:, 2, :])
                    for j in range(NT):
                        nc.vector.tensor_scalar(rows_l[:, j, :], rows_l[:, j, :], nrm[:, 1, j:j + 1], None,
                                                ALU.mult).then_inc(zn_done, 1)
                    link(nc.vector.tensor_scalar(ss[:, 1, :], ss[:, 1, :], -0.5, None, ALU.mult))
                    for j in range(NT):
                        nc.vector.tensor_scalar(K[:, j * P:(j + 1) * P], ident[:, :], ss[:, 1, j:j + 1], None,
                                                ALU.mult).then_inc(diag_done, 1)
                    for q in range(2):
                        dve.wait_ge(sq_ps, b * 2 + q + 1)
                        nc.vector.tensor_copy(half_sq[:, q * 512:q * 512 + 512], bank[4 + q][:, :]).then_inc(sq_done, 1)
                    dve.wait_ge(sq_done, b * 2 + 2)
                    dve.wait_ge(adjm_done, NT)
                    for i in range(NT):
                        dve.wait_ge(K_ready, b * NT + i)
                        dve.wait_ge(sim_l, b * NT + i + 1)
                        nc.vector.scalar_tensor_tensor(A[0][:, :], two_banks[0], 0.0, adj_m[:, i, :], ALU.max, ALU.mult,
                                                       accum_out=coef[:, 0:1]).then_inc(l_used, 1)
                        dve.wait_ge(sim_g, b * NT + i + 1)
                        nc.vector.scalar_tensor_tensor(A[1][:, :], two_banks[1], ss[:, 1, i:i + 1], half_sq[:, :],
                                                       ALU.add, ALU.add).then_inc(g_used, 1)
                        dve.wait_ge(exp_done, b * NT + i + 1)
                        dve.wait_ge(l_used, b * NT + i + 1)
                        link(nc.vector.scalar_tensor_tensor(A[1][:, :], A[1][:, :], 1.0, adj_m[:, i, :], ALU.min,
                                                            ALU.mult, accum_out=coef[:, 1:2]))
                        link(nc.vector.tensor_scalar(coef[:, :], coef[:, :], EPS, None, ALU.max))
                        link(nc.vector.reciprocal(coef[:, :], coef[:, :]))
                        link(nc.vector.tensor_tensor(coef[:, :], coef[:, :], gate[:, 2:4], ALU.mult))
                        link(nc.vector.tensor_scalar(A[0][:, :], A[0][:, :], coef[:, 0:1], None, ALU.mult))
                        dve.wait_ge(KT_done, b * (2 * NT) + 2 * i)
                        nc.vector.scalar_tensor_tensor(K[:, :], A[1][:, :], coef[:, 1:2], A[0][:, :],
                                                       ALU.mult, ALU.add).then_inc(K_ready, 1)
                        if i:
                            out_rows(dve, b, i - 1)
                    out_rows(dve, b, NT - 1)
                    assert nlink[0] == LINKS, nlink[0]

            @block.tensor
            def _(pe):
                def mm(dst, pairs):
                    for n, (l, r) in enumerate(pairs):
                        last = nc.tensor.matmul(dst, l, r, start=n == 0, stop=n == len(pairs) - 1)
                    return last

                pe.wait_ge(w_in, 64)
                for n in range(12):
                    if n >= 8:
                        pe.wait_ge(gw_done, n - 7)
                    src, k = raw[(0, 1, 3)[n // 4]], n % 4
                    for m in range(KD):
                        last = nc.tensor.transpose(bank[n % 8][:, m * P:(m + 1) * P], src[:, m, k * P:(k + 1) * P],
                                                   ident[:, :])
                    last.then_inc(gw_ps, 1)
                pe.wait_ge(gw_done, 12)
                for m in range(KD):
                    mm(bank[(12 + m) % 8][:, :], [(raw[2][:, k, m * P:(m + 1) * P], woT[:, k, :])
                                                  for k in range(KD)]).then_inc(gw_ps, 1)
                pe.wait_ge(gw_done, 16)
                with pe.Fori(0, B) as b:
                    pe.wait_ge(o_done, b * NT)
                    for i in range(8):
                        if i == 0:
                            pe.wait_ge(ln_done, b * NT + 4)
                        if i == 4:
                            pe.wait_ge(ln_done, b * NT + 8)
                        for j in range(4):
                            r = (i // 4) * 4 + j
                            last = nc.tensor.transpose(bank[i][:, j * P:(j + 1) * P],
                                                       rows_l[:, r, (i % 4) * P:(i % 4 + 1) * P], ident[:, :])
                        last.then_inc(hT_ps, 1)
                    pe.wait_ge(hT_done, b * 8 + 8)
                    for n in range(2 * NT):
                        if n >= 8:
                            pe.wait_ge(z_squared, b * (2 * NT) + n - 7)
                        mm(bank[n % 8][:, :], [(hT[:, k, (n % NT) * P:(n % NT + 1) * P], wT[n // NT][:, k, :])
                                               for k in range(KD)]).then_inc(z_ps, 1)
                    pe.wait_ge(z_squared, b * (2 * NT) + 2 * NT)
                    pe.wait_ge(diag_done, b * NT + NT)
                    for q in range(2):
                        for j in range(4):
                            last = nc.tensor.matmul(bank[4 + q][:, j * P:(j + 1) * P], ones[:, :],
                                                    K[:, (4 * q + j) * P:(4 * q + j + 1) * P],
                                                    start=j == 0, stop=True, skip_group_check=True)
                        last.then_inc(sq_ps, 1)
                    pe.wait_ge(sq_done, b * 2 + 2)
                    pe.wait_ge(zn_done, b * NT + NT)
                    for n in range(16):
                        if n >= 4:
                            pe.wait_ge(zT_done, b * 16 + n - 3)
                        for j in range(4):
                            r = (n % 8 // 4) * 4 + j
                            last = nc.tensor.transpose(bank[4 + n % 4][:, j * P:(j + 1) * P],
                                                       (rows_l, rows_g)[n // 8][:, r, (n % 4) * P:(n % 4 + 1) * P],
                                                       ident[:, :])
                        last.then_inc(zT_ps, 1)
                    pe.wait_ge(zT_done, b * 16 + 16)
                    for i in range(NT):
                        if i >= 4:
                            pe.wait_ge(v_done, b * NT + i - 3)
                        mm(bank[i % 4][:, :], [(hT[:, k, i * P:(i + 1) * P], wT[2][:, k, :])
                                               for k in range(KD)]).then_inc(v_ps, 1)
                    pe.wait_ge(v_done, b * NT + NT)

                    def sims(i):
                        for z, (ready, used) in enumerate(((sim_l, l_used), (sim_g, g_used))):
                            pe.wait_ge(used, b * NT + i)
                            for q in range(2):
                                last = mm(bank[2 * z + q], [(zT[z][:, k, i * P:(i + 1) * P],
                                                             zT[z][:, k, q * 512:q * 512 + 512]) for k in range(KD)])
                            last.then_inc(ready, 1)

                    def apply(i):
                        pe.wait_ge(K_ready, b * NT + i + 1)
                        for q in range(2):
                            for j in range(4):
                                last = nc.tensor.transpose(bank[4 + q][:, j * P:(j + 1) * P],
                                                           K[:, (4 * q + j) * P:(4 * q + j + 1) * P], ident[:, :])
                            last.then_inc(KT_ps, 1)
                        pe.wait_ge(KT_done, b * (2 * NT) + 2 * i + 2)
                        if i >= 2:
                            pe.wait_ge(o_done, b * NT + i - 1)
                        mm(bank[6 + i % 2], [(KT[:, j * P:(j + 1) * P], v[:, j, :])
                                             for j in range(NT)]).then_inc(o_ps, 1)

                    sims(0)
                    for i in range(NT):
                        if i + 1 < NT:
                            sims(i + 1)
                        apply(i)


_INS = ['x', 'adj', 'L0_gnn_b1', 'L0_gnn_W2', 'L0_gnn_b2', 'L1_gnn_W_lang', 'L1_gnn_W_grav', 'L1_gnn_W_V',
        'L1_gnn_W_O', 'L1_gnn_gate_logit', 'L1_gnn_log_sigma']


def kernel(**inputs):
    import numpy as np
    import concourse.bacc as bacc
    from concourse.bass_utils import run_bass_kernel_spmd

    nc = bacc.Bacc("TRN2", target_bir_lowering=False, num_devices=1)
    arrays, args = {}, []
    for name in _INS:
        a = np.ascontiguousarray(inputs[name])
        if a.ndim == 0:
            a = a.reshape(1)
        arrays[f"in_{name}"] = a
        args.append(nc.dram_tensor(f"in_{name}", a.shape, mybir.dt.from_np(a.dtype), kind="ExternalInput").ap())
    args.append(nc.dram_tensor("out", (B, T, D), F32, kind="ExternalOutput").ap())
    build(nc, *args)
    r = run_bass_kernel_spmd(nc, [arrays], core_ids=[0])
    return r.results[0]["out"]
```
